# Optimizing a Trainium2 kernel written in Bass

```python
import numpy as np
import jax
import jax.numpy as jnp

def _softmax(x, axis=-1):
    return jax.nn.softmax(x, axis=axis)

def _gelu(x):
    return jax.nn.gelu(x, approximate=True)

def _silu(x):
    return jax.nn.silu(x)

def _sigmoid(x):
    return jax.nn.sigmoid(x)

def _layernorm(x, axis=-1, eps=1e-05):
    m = jnp.mean(x, axis=axis, keepdims=True)
    v = jnp.var(x, axis=axis, keepdims=True)
    return (x - m) / jnp.sqrt(v + eps)

def _scatter_add(tgt, idx, src, axis=0):
    return tgt.at[idx].add(src)

def _segment_sum(src, seg, n):
    return jax.ops.segment_sum(src, seg, n)
kernel_name = 'mk_decoder_postln_d1_seqx_r8_1c3205'

def setup_inputs(seed: int=0):
    np.random.seed(seed)
    _w = jnp.asarray

    def _rec_inputs():
        import jax
        import jax.numpy as jnp
        _rk = jax.random.key(seed)
        x = 0.5 + 0.2887 * jax.random.normal(jax.random.fold_in(_rk, 1), (4, 256, 256), jnp.float32)
        _lenS = 256 - jax.random.randint(jax.random.fold_in(_rk, 7), (4,), 0, max(1, 256 // 4) + 1, jnp.int32)
        _lenS2 = 256 - jax.random.randint(jax.random.fold_in(_rk, 8), (4,), 0, max(1, 256 // 4) + 1, jnp.int32)
        _ctx_512P = jax.random.normal(jax.random.fold_in(_rk, 11), (4, 16, 64), jnp.float32)
        _ctx_512c = jax.random.dirichlet(jax.random.fold_in(_rk, 511), 0.3 * jnp.ones((16,), jnp.float32), (4, 256))
        _ctx_512t = jnp.einsum('bsk,bkd->bsd', _ctx_512c, _ctx_512P)
        _ctx_512t = _ctx_512t * jax.lax.rsqrt(jnp.mean(jnp.square(_ctx_512t)) + 1e-12) * 0.953939
        ctx_512 = -0.000392918 + 0.999932 * (_ctx_512t + 0.3 * jax.random.normal(jax.random.fold_in(_rk, 611), (4, 256, 64), jnp.float32))
        return (x, ctx_512)
    x, ctx_512 = _rec_inputs()

    def _L0_attn_setup():
        import jax, jax.numpy as jnp
        import numpy as np
        FP8_MAX = 448.0
        NUM_HEADS = 16

        def act_quant(x):
            scale = jnp.max(jnp.abs(x)) / FP8_MAX
            q = (x / scale).astype(jnp.float8_e4m3fn)
            return (q, scale)
        key = jax.random.key(seed)
        k1, k2, k3, k4 = jax.random.split(key, 4)
        B, S, H = (2, 256, 256)
        x = jax.random.normal(k1, (B, S, H), dtype=jnp.float32)
        W_qkv = jax.random.normal(k2, (H, 3 * H), dtype=jnp.float32) * (1.0 / np.sqrt(H))
        W_out = jax.random.normal(k3, (H, H), dtype=jnp.float32) * (1.0 / np.sqrt(H))
        b_out = jnp.zeros((H,), dtype=jnp.float32)
        return {'x': x, 'W_qkv': W_qkv, 'W_out': W_out, 'b_out': b_out}
    _L0_attn_all = _L0_attn_setup()
    _L0_attn_in = {k: v for k, v in _L0_attn_all.items() if k in ('W_qkv', 'W_out', 'b_out')}
    del _L0_attn_all

    def _L0_xattn_setup():
        import jax, jax.numpy as jnp
        import numpy as np
        B, N, D = (16, 256, 64)
        H = 4
        TOP_K_RATIO = 0.3
        key = jax.random.key(seed)
        k1, k2, k3, k4 = jax.random.split(key, 4)
        h = jax.random.normal(k1, (B, N, D), dtype=jnp.float32)
        adj_raw = jax.random.uniform(k2, (B, N, N), dtype=jnp.float32)
        lim = 1.0 / np.sqrt(D)
        Wq = jax.random.uniform(k3, (D, D), minval=-lim, maxval=lim, dtype=jnp.float32)
        Wk = jax.random.uniform(k4, (D, D), minval=-lim, maxval=lim, dtype=jnp.float32)
        gamma_raw = jnp.float32(-0.85)
        return {'h': h, 'adj_raw': adj_raw, 'Wq': Wq, 'Wk': Wk, 'gamma_raw': gamma_raw}
    _L0_xattn_all = _L0_xattn_setup()
    _L0_xattn_in = {k: v for k, v in _L0_xattn_all.items() if k in ('Wq', 'Wk', 'gamma_raw')}
    del _L0_xattn_all

    def _L0_ffn_setup():
        import jax, jax.numpy as jnp
        import numpy as np
        N_EXPERTS = 8
        TOP_K = 2
        C = 256
        H = 128
        HS = 256
        B, T = (1, 64)
        SCALE = 0.02
        key = jax.random.key(seed)
        ks = jax.random.split(key, 10)
        x = jax.random.normal(ks[0], (B, T, C), dtype=jnp.float32)
        gate_w = jax.random.normal(ks[1], (N_EXPERTS, C), dtype=jnp.float32) * SCALE
        w_gate = jax.random.normal(ks[2], (N_EXPERTS, H, C), dtype=jnp.float32) * SCALE
        w_up = jax.random.normal(ks[3], (N_EXPERTS, H, C), dtype=jnp.float32) * SCALE
        w_down = jax.random.normal(ks[4], (N_EXPERTS, C, H), dtype=jnp.float32) * SCALE
        sh_gate = jax.random.normal(ks[5], (HS, C), dtype=jnp.float32) * SCALE
        sh_up = jax.random.normal(ks[6], (HS, C), dtype=jnp.float32) * SCALE
        sh_down = jax.random.normal(ks[7], (C, HS), dtype=jnp.float32) * SCALE
        se_gate_w = jax.random.normal(ks[8], (1, C), dtype=jnp.float32) * SCALE
        return {'x': x, 'gate_w': gate_w, 'w_gate': w_gate, 'w_up': w_up, 'w_down': w_down, 'sh_gate': sh_gate, 'sh_up': sh_up, 'sh_down': sh_down, 'se_gate_w': se_gate_w}
    _L0_ffn_all = _L0_ffn_setup()
    _L0_ffn_in = {k: v for k, v in _L0_ffn_all.items() if k in ('gate_w', 'w_gate', 'w_up', 'w_down', 'sh_gate', 'sh_up', 'sh_down', 'se_gate_w')}
    del _L0_ffn_all
    return {'x': x, 'ctx_512': ctx_512, 'L0_attn_W_qkv': _L0_attn_in['W_qkv'], 'L0_attn_W_out': _L0_attn_in['W_out'], 'L0_attn_b_out': _L0_attn_in['b_out'], 'L0_xattn_Wq': _L0_xattn_in['Wq'], 'L0_xattn_Wk': _L0_xattn_in['Wk'], 'L0_xattn_gamma_raw': _L0_xattn_in['gamma_raw'], 'L0_ffn_gate_w': _L0_ffn_in['gate_w'], 'L0_ffn_w_gate': _L0_ffn_in['w_gate'], 'L0_ffn_w_up': _L0_ffn_in['w_up'], 'L0_ffn_w_down': _L0_ffn_in['w_down'], 'L0_ffn_sh_gate': _L0_ffn_in['sh_gate'], 'L0_ffn_sh_up': _L0_ffn_in['sh_up'], 'L0_ffn_sh_down': _L0_ffn_in['sh_down'], 'L0_ffn_se_gate_w': _L0_ffn_in['se_gate_w']}

def reference(x, ctx_512, L0_attn_W_qkv, L0_attn_W_out, L0_attn_b_out, L0_xattn_Wq, L0_xattn_Wk, L0_xattn_gamma_raw, L0_ffn_gate_w, L0_ffn_w_gate, L0_ffn_w_up, L0_ffn_w_down, L0_ffn_sh_gate, L0_ffn_sh_up, L0_ffn_sh_down, L0_ffn_se_gate_w):
    import jax
    import jax.numpy as jnp

    def _L0_attn_ref(x, W_qkv, W_out, b_out):
        import jax, jax.numpy as jnp
        import numpy as np
        FP8_MAX = 448.0
        NUM_HEADS = 16

        def act_quant(x):
            scale = jnp.max(jnp.abs(x)) / FP8_MAX
            q = (x / scale).astype(jnp.float8_e4m3fn)
            return (q, scale)
        B, S, H = x.shape
        nH = NUM_HEADS
        hd = H // nH
        qkv = jnp.einsum('bsh,hf->bsf', x, W_qkv)
        qkv = qkv.reshape(B, S, 3, nH, hd)
        q = qkv[:, :, 0].transpose(0, 2, 1, 3)
        k = qkv[:, :, 1].transpose(0, 2, 1, 3)
        v = qkv[:, :, 2].transpose(0, 2, 1, 3)
        q8, q_scale = act_quant(q)
        k8, k_scale = act_quant(k)
        scores = jnp.einsum('bhqd,bhkd->bhqk', q8.astype(jnp.float32), k8.astype(jnp.float32))
        scores = scores * (q_scale * k_scale) / jnp.sqrt(jnp.float32(hd))
        attn = jax.nn.softmax(scores, axis=-1)
        v8, v_scale = act_quant(v)
        out = jnp.einsum('bhqk,bhkd->bhqd', attn, v8.astype(jnp.float32))
        out = out * v_scale
        out = out.transpose(0, 2, 1, 3).reshape(B, S, H)
        return jnp.einsum('bsh,ho->bso', out, W_out) + b_out

    def _L0_xattn_ref(h, adj_raw, Wq, Wk, gamma_raw):
        import jax, jax.numpy as jnp
        import numpy as np
        B, N, D = (16, 256, 64)
        H = 4
        TOP_K_RATIO = 0.3
        b, n, dm = h.shape
        d = dm // H
        Q = (h @ Wq.T).reshape(b, n, H, d).transpose(0, 2, 1, 3)
        K = (h @ Wk.T).reshape(b, n, H, d).transpose(0, 2, 1, 3)
        sim = jnp.einsum('bhnd,bhmd->bnm', Q, K) / (jnp.sqrt(jnp.float32(d)) * H)
        k = max(1, int(n * TOP_K_RATIO))
        topk_vals = jax.lax.top_k(sim, k)[0]
        threshold = topk_vals[:, :, -1:]
        sparse_mask = (sim >= threshold).astype(sim.dtype)
        A_learned = jax.nn.sigmoid(sim) * sparse_mask
        A_learned = (A_learned + jnp.swapaxes(A_learned, -1, -2)) * 0.5
        gamma = jax.nn.sigmoid(gamma_raw)
        return (1.0 - gamma) * adj_raw + gamma * A_learned

    def _L0_ffn_ref(x, gate_w, w_gate, w_up, w_down, sh_gate, sh_up, sh_down, se_gate_w):
        import jax, jax.numpy as jnp
        import numpy as np
        N_EXPERTS = 8
        TOP_K = 2
        C = 256
        H = 128
        HS = 256
        B, T = (1, 64)
        SCALE = 0.02
        Bb, Tt, Cc = x.shape
        xf = x.reshape(-1, Cc)
        scores = xf @ gate_w.T
        ew, ei = jax.lax.top_k(scores, TOP_K)
        ew = jax.nn.softmax(ew, axis=-1)
        x1 = jax.nn.silu(jnp.einsum('td,ehd->teh', xf, w_gate))
        x3 = jnp.einsum('td,ehd->teh', xf, w_up)
        expert_out = jnp.einsum('teh,edh->ted', x1 * x3, w_down)
        onehot = jax.nn.one_hot(ei, N_EXPERTS, dtype=ew.dtype)
        comb = jnp.einsum('ta,tae->te', ew, onehot)
        routed = jnp.einsum('te,ted->td', comb, expert_out)
        shared = jax.nn.silu(xf @ sh_gate.T) * (xf @ sh_up.T) @ sh_down.T
        sgate = jax.nn.sigmoid(xf @ se_gate_w.T)
        return (routed + sgate * shared).reshape(Bb, Tt, Cc)
    x = _layernorm(x + _L0_attn_ref(x, L0_attn_W_qkv, L0_attn_W_out, L0_attn_b_out), axis=-1)
    x = _layernorm(x + _L0_xattn_ref(ctx_512, x, L0_xattn_Wq, L0_xattn_Wk, L0_xattn_gamma_raw), axis=-1)
    x = _layernorm(x + _L0_ffn_ref(x, L0_ffn_gate_w, L0_ffn_w_gate, L0_ffn_w_up, L0_ffn_w_down, L0_ffn_sh_gate, L0_ffn_sh_up, L0_ffn_sh_down, L0_ffn_se_gate_w), axis=-1)
    return x

_drawn_inputs = setup_inputs


def setup_inputs(seed=0):
    import zlib

    import numpy as np

    out = dict(_drawn_inputs(seed))
    spreads = {'L0_attn_b_out': (0.0, 0.1)}
    factors = {'L0_ffn_gate_w': 5.793,
     'L0_ffn_w_gate': 5.689,
     'L0_ffn_w_up': 5.494,
     'L0_ffn_w_down': 5.516,
     'L0_ffn_sh_gate': 6.431,
     'L0_ffn_sh_up': 6.167,
     'L0_ffn_sh_down': 5.57,
     'L0_ffn_se_gate_w': 8.0}
    for name, (base, spread) in spreads.items():
        noise = np.random.default_rng([zlib.crc32(name.encode()), seed]).standard_normal(out[name].shape)
        drawn = base * np.exp(spread * noise) if base else spread * noise
        out[name] = jnp.asarray(drawn.astype(out[name].dtype))
    for name, factor in factors.items():
        out[name] = (out[name] * factor).astype(out[name].dtype)
    return out
```

```python
from contextlib import ExitStack

import concourse.bass as bass
from concourse import mybir

F32 = mybir.dt.float32
BF16 = mybir.dt.bfloat16
I32 = mybir.dt.int32
U32 = mybir.dt.uint32
ALU = mybir.AluOpType
ACT = mybir.ActivationFunctionType
AX = mybir.AxisListType

P = 128
FP8_MAX = 448.0
LN_EPS = 1e-5
TOP_K_RATIO = 0.3
E4M3_LEAST_NORMAL = 2.0 ** -6
E4M3_ROUNDER = 1.5 * 2.0 ** 20
EXPONENT_BITS = 0x7F800000
LOWEST = -3.0e38


def decoder_layer(nc, x, ctx_512, W_qkv, W_out, b_out, Wq, Wk, gamma_raw, gate_w, w_gate, w_up, w_down,
                  sh_gate, sh_up, sh_down, se_gate_w, out):
    B, S, C = x.shape
    TOK = B * S
    NT = TOK // P
    QT = S // P
    KC = C // P
    NH = 16
    HD = C // NH
    HG = P // HD
    D = ctx_512.shape[2]
    SIM_HEADS = 4
    SIM_SCALE = 1.0 / ((D // SIM_HEADS) ** 0.5 * SIM_HEADS)
    TOPK = max(1, int(S * TOP_K_RATIO))
    ROUNDS = (TOPK + 7) // 8
    NE, HM, _ = w_gate.shape
    HS = sh_gate.shape[0]
    NS = HS // P
    NF = NE + NS
    NW = NE + 1
    SLOT = 32
    NG = NH // 4
    ER = 8
    NSF = KC * QT * HG // 2
    assert HM == P and QT == 2 and KC == 2 and D == 64

    es = ExitStack()
    with es:
        def sb(name, shape, dt=F32):
            return es.enter_context(nc.sbuf_tensor(name, shape, dt))

        def sem(name):
            return es.enter_context(nc.semaphore(name))

        x_sb = sb("x_sb", [P, NT, C])
        ctx_sb = sb("ctx_sb", [P, NT, D])
        wc_sb = sb("wc_sb", [D, 2, D])
        place_qkv = sb("wqkv_avT_attn", [P, 3 * KC * C])
        wqkv = place_qkv[:].rearrange("p (k f) -> p k f", k=KC)
        wout = sb("wout", [P, KC, C])
        bout = sb("bout", [P, C])
        place_gu = sb("wgu_expo_silu", [P, 2 * NF * C])
        wg_nat = place_gu[:, 0:NF * C].rearrange("p (f c) -> p f c", f=NF)
        wu_nat = place_gu[:, NF * C:2 * NF * C].rearrange("p (f c) -> p f c", f=NF)
        place_d = sb("wd_hid", [P, NF * C])
        wd_nat = place_d[:].rearrange("p (k f h) -> p k f h", k=KC, f=NF)
        gw_nat = sb("gw_nat", [NW, C])
        graw = sb("graw", [P, 1])

        ident = sb("ident", [P, P])
        identb = sb("identb", [P, P], BF16)
        ones = sb("ones", [P, P])
        headmask = sb("headmask", [P, HG])
        sel = sb("sel", [P, NH, P], BF16)
        iota = sb("iota", [P, NE])
        halfneg = sb("halfneg", [P, QT])
        wcT = sb("wcT", [P, 2, P])
        place_t = sb("xT_ctxT_qkcT_wgT_wuT", [P, 5 * TOK])
        xT = place_t[:, 0:KC * TOK].rearrange("p (k s) -> p k s", k=KC)
        ctxT = place_t[:, KC * TOK:(KC + 1) * TOK]
        qkcT = place_t[:, (KC + 1) * TOK:(KC + 3) * TOK].rearrange("p (k s) -> p k s", k=2)
        sim = sb("sim", [P, NT, S])
        work = sb("work", [P, QT, S])
        top8 = sb("top8", [P, QT, 8])
        sig = sb("sig", [P, QT, S])
        adj = sb("adj", [P, QT, S])
        adjs = sb("adjs", [P, QT, S])
        gam = sb("gam", [P, 5])

        qkraw = sb("qkraw", [P, 2, KC, TOK])
        vraw = sb("vraw", [P, NT, C])
        amax = sb("amax", [P, 3, 4])
        amax3 = sb("amax3", [P, 3])
        gmax = sb("gmax", [3, 1])
        gdiag = sb("gdiag", [3, 3])
        scale3 = sb("scale3", [P, 3])
        inv3 = sb("inv3", [P, 3])
        cexp = sb("cexp", [P, 1])

        qs = sb("qs", [P, 3, 2 * S])
        qm = sb("qm", [P, 3, 2 * S])
        k8 = sb("k8", [P, KC, S], BF16)
        q8 = sb("q8", [P, 2, KC, S], BF16)
        kmask = sb("kmask", [P, 2, NH, S], BF16)
        v8 = sb("v8", [P, 2, QT, NH, SLOT])
        negm = sb("negm", [P, QT, NH])
        mparts = sb("mparts", [P, QT, P], BF16)
        mT = sb("mT", [P, 2, S], BF16)
        expo = place_gu[:, 0:ER * QT * S].rearrange("p (h t s) -> p h t s", h=ER, t=QT)
        avT = place_qkv[:, 0:NG * S].rearrange("p (g s) -> p g s", g=NG)
        rsum = sb("rsum", [P, QT, NH])
        attn = place_qkv[:, NG * S:NG * S + QT * C].rearrange("p (t c) -> p t c", t=QT)
        aT = sb("aT", [P, KC, S])
        pre1 = sb("pre1", [P, QT, C])
        pre2 = sb("pre2", [P, QT, C])
        x2 = sb("x2", [P, 2, QT, C])
        yo = sb("yo", [P, 2, QT, C])
        stats = sb("stats", [P, 3, QT, 6])
        mv = sb("mv", [P, 3, QT, 2])
        vare = sb("vare", [P, 3, QT])
        rstd = sb("rstd", [P, 3, QT])
        rg = sb("rg", [P, QT])

        wgT = place_t[:, 0:KC * NF * P].rearrange("p (k f h) -> p k f h", k=KC, f=NF)
        wuT = place_t[:, KC * NF * P:2 * KC * NF * P].rearrange("p (k f h) -> p k f h", k=KC, f=NF)
        wdT = sb("wdT", [P, NF, C])
        gwT = sb("gwT", [P, KC, NW])
        x2T = sb("x2T", [P, 2, KC, S])
        rsc = sb("rsc", [P, QT, NW])
        rtop = sb("rtop", [P, QT, 8])
        ridx = sb("ridx", [P, QT, 8], U32)
        ridf = sb("ridf", [P, QT, 2])
        rarg = sb("rarg", [P, QT, 2])
        rexp = sb("rexp", [P, QT, 2])
        rden = sb("rden", [P, QT, 2])
        rw = sb("rw", [P, QT, 2])
        rw2 = sb("rw2", [P, QT, 1])
        hot = sb("hot", [P, QT, 2, NE])
        comb = sb("comb", [P, QT, NW])
        combT = sb("combT", [NW, S])
        cb = sb("cb", [P, NW, S])
        silu = place_gu[:, ER * QT * S:ER * QT * S + 4 * S].rearrange("p (n f s) -> p n f s", n=2, f=2)
        hid1 = sb("hid1", [P, 2, 2, S])
        hid = place_d[:].rearrange("p (f s) -> p f s", f=NF)
        comb_dram = nc.dram_tensor("comb_dram", (B, NW, S), F32, kind="Internal").ap()

        bank = {n: es.enter_context(nc.psum_tensor(n, [P, 512], F32))
                for n in ("SA0", "SA1", "ST0", "ST1", "AV0", "AV1", "MG", "MU")}

        filled = {n: sem("filled_" + n) for n in bank}
        emptied = {n: sem("emptied_" + n) for n in bank}
        place, count = {}, {n: 0 for n in bank}

        def plan(key, name):
            place[key] = (name, count[name])
            count[name] += 1

        four = ("AV0", "AV1", "MG", "MU")
        plan(("cw",), "SA0")
        for hf in range(2):
            plan(("ct", hf), ("SA1", "ST0")[hf])
        for kind in range(2):
            for hf in range(2):
                plan(("cq", kind, hf), ("SA0", "ST1")[hf])
        for b in range(B):
            plan(("sim", b), ("SA1", "ST0")[b % 2])
        for n in range(4):
            plan(("xt", n), four[n])
        for n in range(8):
            plan(("qk", n), four[n % 4])
        for n in range(4):
            plan(("v", n), four[n])
        plan(("mx", 0), "ST1")
        plan(("mx", 1), "ST1")
        NWT = 3 * KC * NF // 4
        for n in range(NWT):
            plan(("wt", n), four[n % 4])
        plan(("gw",), "AV0")
        for b in range(B):
            for i in range(NSF):
                plan(("s", b, i), ("SA0", "SA1")[i % 2])
            plan(("mT", b), "SA0")
            for h in range(NH):
                plan(("st", b, h), ("ST0", "ST1")[h % 2])
        for b in range(B + 1):
            if b == 0:
                plan(("at", 0), "MG")
            if b < B:
                for i in range(2):
                    plan(("av", b, i), ("AV0", "AV1")[i])
                for t in range(QT):
                    plan(("avt", b, t), ("AV0", "AV1")[t])
                plan(("aT", b), "AV0")
                plan(("op", b), "AV1")
            if b > 0:
                for f in range(NF // 2):
                    plan(("g", b - 1, f), "MG")
                    plan(("u", b - 1, f), "MU")
                plan(("y", b - 1), "MG")
            if b + 1 < B:
                plan(("at", b + 1), "AV0")
            if b < B:
                plan(("x2t", b), "MU")
                plan(("rt", b), "AV0")
                plan(("cT", b), "AV1")

        def begin_fill(pe, key):
            name, n = place[key]
            if n:
                pe.wait_ge(emptied[name], n)
            return bank[name]

        def end_fill(ins, key):
            ins.then_inc(filled[place[key][0]], 1)

        def full(eng, key):
            name, n = place[key]
            eng.wait_ge(filled[name], n + 1)
            return bank[name]

        def release(ins, key):
            ins.then_inc(emptied[place[key][0]], 1)

        def read_out(eng, key):
            name, n = place[key]
            eng.wait_ge(emptied[name], n + 1)

        ld_ctx, ld_wc, ld_wqkv, ld_small = sem("ld_ctx"), sem("ld_wc"), sem("ld_wqkv"), sem("ld_small")
        ld_x = [sem(f"ld_x{i}") for i in range(2)]
        ld_wg, ld_wu, ld_wd, ld_gw, ld_wout = sem("ld_wg"), sem("ld_wu"), sem("ld_wd"), sem("ld_gw"), sem("ld_wout")
        const_step, consts = sem("const_step"), sem("consts")
        bias_added = sem("bias_added")
        gate_exp = sem("gamma_exp")
        tanh_done, topk_step, adj_done = sem("tanh_done"), sem("topk_step"), sem("adj_done")
        amax_done, gmax_done = sem("amax_done"), sem("gmax_done")
        scales_done = sem("scales_done")
        scaled, expbits, rounder = sem("scaled"), sem("expbits"), sem("rounder")
        q8_done, k8_done, km_done, v_step = sem("q8_done"), sem("k8_done"), sem("kmask_done"), sem("v_step")
        mparts_done = sem("mparts_done")
        av_half = sem("av_half")
        attn_done = sem("attn_done")
        mv_s = [sem(f"mean_var{i}_done") for i in range(3)]
        ve_s = [sem(f"var_eps{i}_done") for i in range(3)]
        rstd_s = [sem(f"rstd{i}_done") for i in range(3)]
        x2_done = sem("x2_done")
        rarg_done, rexp_done, comb_done = sem("router_arg_done"), sem("router_exp_done"), sem("comb_done")
        comb_written, cb_done = sem("comb_written"), sem("cb_done")
        silu_done, hid_done = sem("silu_done"), sem("hid_done")
        yo_done, out_done = sem("yo_done"), [sem(f"out_done{i}") for i in range(2)]
        dve_step = sem("dve_step")

        NP2 = NF // 2
        block = es.enter_context(nc.Block())

        @block.sync
        def _(sp):
            sp.dma_start(ctx_sb[:], ctx_512.rearrange("b (t p) d -> p (b t) d", p=P)).then_inc(ld_ctx, 16)
            sp.dma_start(wc_sb[:, 0, :], Wq).then_inc(ld_wc, 16)
            sp.dma_start(wc_sb[:, 1, :], Wk).then_inc(ld_wc, 16)
            xv = x.rearrange("b (t p) c -> p (b t) c", p=P)
            sp.dma_start(x_sb[:, 0:NT // 2, :], xv[:, 0:NT // 2, :]).then_inc(ld_x[0], 16)
            sp.dma_start(wqkv[:], W_qkv.rearrange("(k p) f -> p k f", p=P)).then_inc(ld_wqkv, 16)
            sp.dma_start(x_sb[:, NT // 2:NT, :], xv[:, NT // 2:NT, :]).then_inc(ld_x[1], 16)
            sp.dma_start(graw[:], gamma_raw.rearrange("(a c) -> a c", a=1).broadcast_to((P, 1))).then_inc(ld_small, 16)
            sp.dma_start(bout[:], b_out.rearrange("(a c) -> a c", a=1).broadcast_to((P, C))).then_inc(ld_small, 16)
            sp.dma_start(wg_nat[:, 0:NE, :], w_gate.rearrange("e h c -> h e c")).then_inc(ld_wg, 16)
            sp.dma_start(wg_nat[:, NE:NF, :], sh_gate.rearrange("(s h) c -> h s c", h=P)).then_inc(ld_wg, 16)
            sp.dma_start(wu_nat[:, 0:NE, :], w_up.rearrange("e h c -> h e c")).then_inc(ld_wu, 16)
            sp.dma_start(wu_nat[:, NE:NF, :], sh_up.rearrange("(s h) c -> h s c", h=P)).then_inc(ld_wu, 16)
            for k in range(KC):
                sp.dma_start(wd_nat[:, k, 0:NE, :], w_down[:, k * P:(k + 1) * P, :].rearrange("e c h -> c e h")).then_inc(ld_wd, 16)
                sp.dma_start(wd_nat[:, k, NE:NF, :], sh_down[k * P:(k + 1) * P, :].rearrange("c (s h) -> c s h", h=P)).then_inc(ld_wd, 16)
            sp.dma_start(gw_nat[0:NE, :], gate_w).then_inc(ld_gw, 16)
            sp.dma_start(gw_nat[NE:NW, :], se_gate_w).then_inc(ld_gw, 16)
            sp.dma_start(wout[:], W_out.rearrange("(k p) o -> p k o", p=P)).then_inc(ld_wout, 16)
            for b in range(B + 1):
                if b >= 1:
                    sp.wait_ge(yo_done, QT * b)
                    sp.dma_start(out[b - 1].rearrange("(t p) c -> p t c", p=P), yo[:, (b - 1) % 2]).then_inc(out_done[(b - 1) % 2], 16)
                if b < B:
                    read_out(sp, ("cT", b))
                    sp.dma_start(comb_dram[b], combT[:]).then_inc(comb_written, 16)
                    sp.wait_ge(comb_written, 16 * (b + 1))
                    if b >= 1:
                        sp.wait_ge(hid_done, NP2 * b)
                    sp.dma_start(cb[:, :, :], comb_dram[b:b + 1].broadcast_to((P, NW, S))).then_inc(cb_done, 16)
            for i in range(2):
                sp.wait_ge(out_done[i], 16 * (B // 2))
            sp.wait_ge(cb_done, 16 * B)

        @block.gpsimd
        def _(pool):
            pool.memset(ident[:], 0.0).then_inc(const_step, 1)
            pool.memset(wcT[:], 0.0).then_inc(consts, 1)
            pool.memset(ctxT, 0.0).then_inc(consts, 1)
            pool.wait_ge(const_step, 1)
            pool.affine_select(out=ident[:], in_=ident[:], compare_op=ALU.not_equal, fill=1.0, base=0,
                               pattern=[[-1, P]], channel_multiplier=1).then_inc(consts, 1)
            pool.memset(identb[:], 0.0).then_inc(const_step, 1)
            pool.memset(headmask[:], 1.0).then_inc(const_step, 1)
            pool.memset(sel[:], 0.0).then_inc(const_step, 1)
            pool.wait_ge(const_step, 4)
            pool.affine_select(out=identb[:], in_=identb[:], compare_op=ALU.not_equal, fill=1.0, base=0,
                               pattern=[[-1, P]], channel_multiplier=1).then_inc(consts, 1)
            pool.affine_select(out=headmask[:], in_=headmask[:], compare_op=ALU.is_ge, fill=0.0, base=0,
                               pattern=[[-HD, HG]], channel_multiplier=1).then_inc(const_step, 1)
            pool.affine_select(out=sel[:], in_=sel[:], compare_op=ALU.not_equal, fill=1.0, base=0,
                               pattern=[[-1, NH], [0, P]], channel_multiplier=1).then_inc(const_step, 1)
            pool.wait_ge(const_step, 6)
            pool.affine_select(out=headmask[:], in_=headmask[:], compare_op=ALU.is_ge, fill=0.0, base=HD - 1,
                               pattern=[[HD, HG]], channel_multiplier=-1).then_inc(consts, 1)
            pool.affine_select(out=sel[:], in_=sel[:], compare_op=ALU.not_equal, fill=1.0, base=-NH,
                               pattern=[[-1, NH], [0, P]], channel_multiplier=1).then_inc(consts, 1)
            pool.memset(ones[:], 1.0).then_inc(consts, 1)
            pool.memset(v8[:], 1.0).then_inc(consts, 1)
            pool.memset(mparts[:], 0.0).then_inc(consts, 1)
            pool.memset(halfneg[:], -0.5).then_inc(const_step, 1)
            pool.wait_ge(consts, 9)
            pool.wait_ge(const_step, 7)

            def quantize(b):
                for kind in range(3):
                    pool.wait_ge(expbits, 3 * b + kind + 1)
                    pool.tensor_scalar(qm[:, kind, :], qm[:, kind, :], E4M3_LEAST_NORMAL, E4M3_ROUNDER,
                                       ALU.max, ALU.mult).then_inc(rounder if kind < 2 else v_step, 1)
                pool.wait_ge(k8_done, b + 1)
                if b >= 2:
                    full(pool, ("st", b - 2, NH - 1))
                for h in range(NH):
                    pool.tensor_scalar(kmask[:, b % 2, h, :], k8[:, h // HG, :], headmask[:, h % HG:h % HG + 1], None,
                                       ALU.mult).then_inc(km_done, 1)
                pool.wait_ge(v_step, 3 * b + 1)
                pool.tensor_tensor(qs[:, 2, :], qs[:, 2, :], qm[:, 2, :], ALU.add).then_inc(v_step, 1)
                pool.wait_ge(v_step, 3 * b + 2)
                if b >= 2:
                    full(pool, ("av", b - 2, 1))
                pool.tensor_tensor(v8[:, b % 2, :, :, 0:HD], qs[:, 2, :].rearrange("p (t h d) -> p t h d", t=QT, h=NH),
                                   qm[:, 2, :].rearrange("p (t h d) -> p t h d", t=QT, h=NH),
                                   ALU.subtract).then_inc(v_step, 1)

            def inv_std(i, n):
                pool.wait_ge(mv_s[i], QT * (n + 1))
                pool.tensor_scalar(vare[:, i, :], mv[:, i, :, 1], LN_EPS, None, ALU.add).then_inc(ve_s[i], 1)
                pool.wait_ge(ve_s[i], n + 1)
                pool.tensor_tensor(rstd[:, i, :], vare[:, i, :], halfneg[:], ALU.pow).then_inc(rstd_s[i], 1)

            def weigh_hidden(b):
                pool.wait_ge(cb_done, 16 * (b + 1))
                if b >= 1:
                    full(pool, ("y", b - 1))
                for f in range(NP2):
                    n = b * NP2 + f
                    read_out(pool, ("u", b, f))
                    for i in range(2):
                        e = min(2 * f + i, NE)
                        ins = pool.tensor_tensor(hid[:, 2 * f + i, :], hid1[:, n % 2, i, :], cb[:, e, :], ALU.mult)
                    ins.then_inc(hid_done, 1)

            quantize(0)
            pool.wait_ge(ld_small, 32)
            for n in range(4):
                full(pool, ("xt", n))
            for t in range(NT):
                pool.tensor_tensor(x_sb[:, t, :], x_sb[:, t, :], bout[:], ALU.add).then_inc(bias_added, 1)
            for b in range(B + 1):
                if b + 1 < B:
                    quantize(b + 1)
                if b < B:
                    inv_std(0, b)
                    inv_std(1, b)
                if b > 0:
                    weigh_hidden(b - 1)
                    inv_std(2, b - 1)

        @block.scalar
        def _(act):
            act.wait_ge(consts, 2)
            src = full(act, ("cw",))
            release(act.copy(wcT[0:D, :, 0:D], src[0:D, 0:2 * D].rearrange("p (k d) -> p k d", k=2)), ("cw",))
            for hf in range(2):
                src = full(act, ("ct", hf))
                release(act.copy(ctxT[0:D, hf * 512:(hf + 1) * 512], src[0:D, :]), ("ct", hf))
            for kind in range(2):
                for hf in range(2):
                    src = full(act, ("cq", kind, hf))
                    release(act.copy(qkcT[:, kind, hf * 512:(hf + 1) * 512], src[:, :]), ("cq", kind, hf))
            for b in range(B):
                src = full(act, ("sim", b))
                release(act.mul(sim[:, QT * b:QT * (b + 1), :], src[:, :].rearrange("p (t s) -> p t s", t=QT), SIM_SCALE), ("sim", b))
            act.wait_ge(ld_small, 32)
            act.activation(gam[:, 0:1], graw[:, :], ACT.Exp, scale=-1.0).then_inc(gate_exp, 1)

            def tanh_sim(b):
                read_out(act, ("sim", b))
                if b >= 1:
                    act.wait_ge(adj_done, QT * b)
                act.activation(sig[:, :, :], sim[:, QT * b:QT * (b + 1), :], ACT.Tanh, scale=0.5).then_inc(tanh_done, 1)

            for n in (0, 2):
                src = full(act, ("xt", n))
                release(act.copy(xT[:, n % 2, (n // 2) * 512:(n // 2 + 1) * 512], src[:, :]), ("xt", n))
            tanh_sim(0)
            for n in range(8):
                hf, kind, g = n // 4, (n // 2) % 2, n % 2
                src = full(act, ("qk", n))
                release(act.copy(qkraw[:, kind, g, hf * 512:(hf + 1) * 512], src[:, :]), ("qk", n))
            for n in range(4):
                src = full(act, ("v", n))
                release(act.copy(vraw[:, 2 * n:2 * n + 2, :], src[:, :].rearrange("p (t c) -> p t c", t=2)), ("v", n))

            def scale_qkv(b):
                act.wait_ge(scales_done, 3)
                for kind in range(3):
                    if b >= 1:
                        act.wait_ge((q8_done, k8_done, v_step)[kind], b if kind < 2 else 3 * b)
                    src = qkraw[:, kind, :, b * S:(b + 1) * S] if kind < 2 else vraw[:, QT * b:QT * (b + 1), :]
                    act.activation(qs[:, kind, :].rearrange("p (t s) -> p t s", t=2), src, ACT.Copy,
                                   scale=inv3[:, kind:kind + 1]).then_inc(scaled, 1)

            scale_qkv(0)
            for n in range(NWT):
                src = full(act, ("wt", n))
                dst = (place_t[:, 0:KC * NF * P], place_t[:, KC * NF * P:2 * KC * NF * P],
                       wdT[:].rearrange("p f c -> p (f c)"))[n // (NWT // 3)]
                m = n % (NWT // 3)
                release(act.copy(dst[:, m * 512:(m + 1) * 512], src[:, :]), ("wt", n))
            src = full(act, ("gw",))
            release(act.copy(gwT[:, :, :], src[:, 0:KC * 16].rearrange("p (k n) -> p k n", k=KC)[:, :, 0:NW]), ("gw",))

            def exponentials(b):
                for h in range(NH):
                    src = full(act, ("st", b, h))
                    grp = (b * NH + h) // 4 - ER // 4
                    if grp >= 0 and grp % 2 == 0:
                        act.wait_ge(av_half, grp // 2 + 1)
                    elif grp >= 0:
                        full(act, ("av", grp // NG, grp % NG // 2))
                    release(act.activation(expo[:, h % ER, :, :], src[:, :].rearrange("p (t s) -> p t s", t=QT), ACT.Exp,
                                           scale=cexp[:, 0:1]), ("st", b, h))
                    if h == NH // 2 + 3:
                        attended(b, 0)
                attended(b, 1)

            def attended(b, i):
                src = full(act, ("av", b, i))
                if b >= 1 and i == 0:
                    full(act, ("avt", b - 1, QT - 1))
                release(act.copy(avT[:, 2 * i:2 * i + 2, :], src[:, :].rearrange("p (g s) -> p g s", g=2)), ("av", b, i))

            for b in range(B + 1):
                if b + 1 < B:
                    scale_qkv(b + 1)
                if b < B:
                    exponentials(b)
                    src = full(act, ("aT", b))
                    if b >= 1:
                        full(act, ("op", b - 1))
                    release(act.copy(aT[:, :, :], src[:, :].rearrange("p (k s) -> p k s", k=KC)), ("aT", b))
                if b + 1 < B:
                    tanh_sim(b + 1)
                if b > 0:
                    for f in range(NP2):
                        n = (b - 1) * NP2 + f
                        src = full(act, ("g", b - 1, f))
                        if n >= 2:
                            read_out(act, ("u", (n - 2) // NP2, (n - 2) % NP2))
                        release(act.activation(silu[:, n % 2, :, :], src[:, :].rearrange("p (f s) -> p f s", f=2),
                                               ACT.Silu), ("g", b - 1, f))
                if b < B:
                    src = full(act, ("x2t", b))
                    release(act.copy(x2T[:, b % 2, :, :], src[:, :].rearrange("p (k s) -> p k s", k=KC)), ("x2t", b))
                    act.wait_ge(rarg_done, 2 * (b + 1))
                    act.activation(rexp[:, :, :], rarg[:, :, :], ACT.Exp).then_inc(rexp_done, 1)
                    src = full(act, ("cT", b))
                    if b >= 1:
                        act.wait_ge(comb_written, 16 * b)
                    release(act.copy(combT[:, :], src[0:NW, 0:S]), ("cT", b))

        @block.vector
        def _(dve):
            steps = [0]

            def step(ins):
                ins.then_inc(dve_step, 1)
                steps[0] += 1
                return steps[0]

            def after(n):
                dve.wait_ge(dve_step, n)

            for e in range(NE):
                dve.memset(iota[:, e:e + 1], float(e))

            def topk_rounds(b, first, last):
                base = b * (4 * ROUNDS - 2)
                if first == 0:
                    read_out(dve, ("sim", b))
                for r in range(first, last):
                    for t in range(QT):
                        if r > 0:
                            dve.wait_ge(topk_step, base + 4 * (r - 1) + 3 + t)
                        src = work[:, t, :] if r else sim[:, QT * b + t, :]
                        dve.max(top8[:, t, :], src).then_inc(topk_step, 1)
                    if r + 1 < ROUNDS:
                        for t in range(QT):
                            dve.wait_ge(topk_step, base + 4 * r + 1 + t)
                            src = work[:, t, :] if r else sim[:, QT * b + t, :]
                            dve.match_replace(work[:, t, :], top8[:, t, :], src, LOWEST).then_inc(topk_step, 1)

            def adjacency(b):
                dve.wait_ge(tanh_done, b + 1)
                after(gamma_step)
                n = step(dve.tensor_scalar(sig[:, :, :], sig[:, :, :], gam[:, 3:4], gam[:, 3:4], ALU.mult, ALU.add))
                dve.wait_ge(topk_step, (b + 1) * (4 * ROUNDS - 2))
                after(n)
                least = (TOPK - 1) % 8
                for t in range(QT):
                    dve.scalar_tensor_tensor(out=adj[:, t, :], in0=sim[:, QT * b + t, :], scalar=top8[:, t, least:least + 1],
                                             in1=sig[:, t, :], op0=ALU.is_ge, op1=ALU.mult).then_inc(adj_done, 1)

            def adjacency_sum(b):
                src = full(dve, ("at", b))
                release(dve.tensor_tensor(adjs[:, :, :], src[:, :].rearrange("p (t s) -> p t s", t=QT),
                                          adj[:, :, :], ALU.add), ("at", b))

            dve.wait_ge(gate_exp, 1)
            n = step(dve.tensor_scalar(gam[:, 1:2], gam[:, 0:1], 1.0, None, ALU.add))
            after(n)
            n = step(dve.reciprocal(gam[:, 2:3], gam[:, 1:2]))
            after(n)
            step(dve.tensor_scalar(gam[:, 3:4], gam[:, 2:3], 0.25, None, ALU.mult))
            gamma_step = step(dve.tensor_scalar(gam[:, 4:5], gam[:, 2:3], -1.0, 2.0, ALU.mult, ALU.add))

            for n in (1, 3):
                src = full(dve, ("xt", n))
                release(dve.tensor_copy(xT[:, n % 2, (n // 2) * 512:(n // 2 + 1) * 512], src[:, :]), ("xt", n))

            def abs_max(kind, j, key, src):
                read_out(dve, key)
                return step(dve.tensor_reduce(amax[:, kind, j:j + 1], src, AX.X, ALU.max, apply_absolute_value=True))

            for n in range(8):
                hf, kind, g = n // 4, (n // 2) % 2, n % 2
                topk_rounds(0, n, n + 1)
                abs_max(kind, 2 * hf + g, ("qk", n), qkraw[:, kind, g, hf * 512:(hf + 1) * 512])
            for n in range(4):
                if n < 2:
                    topk_rounds(0, 8 + n, 9 + n)
                m = abs_max(2, n, ("v", n), vraw[:, 2 * n:2 * n + 2, :].rearrange("p t c -> p (t c)"))
            after(m)
            dve.tensor_reduce(amax3[:, :], amax[:, :, :], AX.X, ALU.max).then_inc(amax_done, 1)
            src = full(dve, ("mx", 0))
            release(dve.tensor_reduce(gmax[:, :], src[0:3, 0:P], AX.X, ALU.max), ("mx", 0))
            read_out(dve, ("mx", 0))
            dve.tensor_scalar(gdiag[:, :], ident[0:3, 0:3], gmax[:, 0:1], None, ALU.mult).then_inc(gmax_done, 1)
            src = full(dve, ("mx", 1))
            release(dve.tensor_scalar(scale3[:, :], src[:, 0:3], 1.0 / FP8_MAX, None, ALU.mult), ("mx", 1))
            read_out(dve, ("mx", 1))
            dve.reciprocal(inv3[:, :], scale3[:, :]).then_inc(scales_done, 1)
            dve.tensor_scalar(cexp[:, :], scale3[:, 0:1], HD ** -0.5, None, ALU.mult).then_inc(scales_done, 1)
            dve.wait_ge(scales_done, 2)
            dve.tensor_scalar(cexp[:, :], cexp[:, :], scale3[:, 1:2], None, ALU.mult).then_inc(scales_done, 1)

            def quantize(b):
                for kind in range(3):
                    dve.wait_ge(scaled, 3 * b + kind + 1)
                    if b >= 1 and kind == 2:
                        dve.wait_ge(v_step, 3 * b)
                    dve.tensor_scalar(qm[:, kind, :].bitcast(I32), qs[:, kind, :].bitcast(I32), EXPONENT_BITS, None,
                                      ALU.bitwise_and).then_inc(expbits, 1)
                for kind in range(2):
                    dve.wait_ge(rounder, 2 * b + kind + 1)
                    n = step(dve.tensor_tensor(qs[:, kind, :], qs[:, kind, :], qm[:, kind, :], ALU.add))
                    after(n)
                    if kind == 0:
                        if b >= 2:
                            full(dve, ("st", b - 2, NH - 1))
                        dst, done = q8[:, b % 2], q8_done
                    else:
                        if b >= 1:
                            dve.wait_ge(km_done, NH * b)
                        dst, done = k8[:, :, :], k8_done
                    dve.tensor_tensor(dst, qs[:, kind, :].rearrange("p (k s) -> p k s", k=KC),
                                      qm[:, kind, :].rearrange("p (k s) -> p k s", k=KC), ALU.subtract).then_inc(done, 1)

            def row_maxima(b, first, last):
                for i in range(first, last):
                    g, t, hp = i // (2 * HG // 2), (i // (HG // 2)) % 2, i % (HG // 2)
                    h = g * HG + 2 * hp
                    src = full(dve, ("s", b, i))
                    release(dve.tensor_reduce(negm[:, t, h:h + 2], src[:, :].rearrange("p (h s) -> p h s", h=2), AX.X,
                                              ALU.max, negate=True), ("s", b, i))

            def split_maxima(b):
                read_out(dve, ("s", b, NSF - 1))
                read_out(dve, ("s", b, NSF - 2))
                if b >= 1:
                    full(dve, ("mT", b - 1))
                dve.tensor_copy(mparts[:, :, 0:NH], negm[:, :, :]).then_inc(mparts_done, 1)
                dve.wait_ge(mparts_done, 2 * b + 1)
                dve.tensor_tensor(mparts[:, :, NH:2 * NH], negm[:, :, :], mparts[:, :, 0:NH], ALU.subtract).then_inc(mparts_done, 1)
                src = full(dve, ("mT", b))
                if b >= 2:
                    full(dve, ("st", b - 2, NH - 1))
                release(dve.tensor_copy(mT[:, b % 2, :], src[:, 0:S // 2].bitcast(BF16)), ("mT", b))

            def statistics(i, src):
                for t in range(QT):
                    n = step(dve.bn_stats(stats[:, i, t, :], src[:, t, :]))
                for t in range(QT):
                    after(n - QT + 1 + t)
                    dve.bn_aggr(mv[:, i, t, :], stats[:, i, t, :]).then_inc(mv_s[i], 1)

            def attention_out(b):
                for t in range(QT):
                    src = full(dve, ("avt", b, t))[:, :].rearrange("p (h s) -> p h s", h=NH)
                    n = step(dve.reciprocal(rsum[:, t, :], src[:, :, HD]))
                    after(n)
                    n = step(dve.tensor_scalar(rsum[:, t, :], rsum[:, t, :], scale3[:, 2:3], None, ALU.mult))
                    after(n)
                    if b >= 1 and t == 0:
                        full(dve, ("aT", b - 1))
                    release(dve.tensor_tensor(attn[:, t, :].rearrange("p (h d) -> p h d", h=NH), src[:, :, 0:HD],
                                              rsum[:, t, :].unsqueeze(2).broadcast_to((P, NH, HD)), ALU.mult), ("avt", b, t))
                src = full(dve, ("op", b))
                dve.wait_ge(bias_added, NT)
                release(dve.tensor_tensor(pre1[:, :, :], src[:, :].rearrange("p (t c) -> p t c", t=QT),
                                          x_sb[:, QT * b:QT * (b + 1), :], ALU.add), ("op", b))
                read_out(dve, ("op", b))
                statistics(0, pre1)
                dve.wait_ge(rstd_s[0], b + 1)
                n = step(dve.tensor_scalar(rg[:, :], rstd[:, 0, :], gam[:, 4:5], None, ALU.mult))
                after(n)
                for t in range(QT):
                    n = step(dve.tensor_scalar(pre1[:, t, :], pre1[:, t, :], mv[:, 0, t, 0:1], rg[:, t:t + 1],
                                               ALU.subtract, ALU.mult))
                after(n)
                n = step(dve.tensor_tensor(pre2[:, :, :], pre1[:, :, :], adjs[:, :, :], ALU.add))
                after(n)
                statistics(1, pre2)
                dve.wait_ge(rstd_s[1], b + 1)
                for t in range(QT):
                    dve.tensor_scalar(x2[:, b % 2, t, :], pre2[:, t, :], mv[:, 1, t, 0:1], rstd[:, 1, t:t + 1],
                                      ALU.subtract, ALU.mult).then_inc(x2_done, 1)

            def hidden(b, f):
                n = b * NP2 + f
                dve.wait_ge(emptied["MG"], place[("g", b, f)][1] + 1)
                if n >= 2:
                    dve.wait_ge(hid_done, n - 1)
                src = full(dve, ("u", b, f))
                release(dve.tensor_tensor(hid1[:, n % 2, :, :], src[:, :].rearrange("p (f s) -> p f s", f=2),
                                          silu[:, n % 2, :, :], ALU.mult), ("u", b, f))

            def experts_out(b):
                src = full(dve, ("y", b))
                release(dve.tensor_tensor(pre1[:, :, :], src[:, :].rearrange("p (t c) -> p t c", t=QT),
                                          x2[:, b % 2], ALU.add), ("y", b))
                read_out(dve, ("y", b))
                statistics(2, pre1)
                dve.wait_ge(rstd_s[2], b + 1)
                if b >= 2:
                    dve.wait_ge(out_done[b % 2], 16 * (b // 2))
                for t in range(QT):
                    dve.tensor_scalar(yo[:, b % 2, t, :], pre1[:, t, :], mv[:, 2, t, 0:1], rstd[:, 2, t:t + 1],
                                      ALU.subtract, ALU.mult).then_inc(yo_done, 1)

            def router(b):
                src = full(dve, ("rt", b))[:, 0:QT * 16].rearrange("p (t n) -> p t n", t=QT)
                release(dve.tensor_copy(rsc[:, :, :], src[:, :, 0:NW]), ("rt", b))
                read_out(dve, ("rt", b))
                for t in range(QT):
                    n = step(dve.max(rtop[:, t, :], rsc[:, t, 0:NE]))
                dve.tensor_scalar(rarg[:, :, 1], rsc[:, :, NE], -1.0, None, ALU.mult).then_inc(rarg_done, 1)
                after(n)
                dve.tensor_tensor(rarg[:, :, 0], rtop[:, :, 1], rtop[:, :, 0], ALU.subtract).then_inc(rarg_done, 1)
                for t in range(QT):
                    n = step(dve.max_index(ridx[:, t, :], rtop[:, t, :], rsc[:, t, 0:NE]))
                after(n)
                n = step(dve.tensor_copy(ridf[:, :, :], ridx[:, :, 0:2]))
                dve.wait_ge(rexp_done, b + 1)
                n = step(dve.tensor_scalar(rden[:, :, :], rexp[:, :, :], 1.0, None, ALU.add))
                after(n)
                n = step(dve.reciprocal(rw[:, :, :], rden[:, :, :]))
                after(n)
                n = step(dve.tensor_tensor(rw2[:, :, 0], rexp[:, :, 0], rw[:, :, 0], ALU.mult))
                after(n)
                for t in range(QT):
                    for j in range(2):
                        w = rw[:, t, 0:1] if j == 0 else rw2[:, t, 0:1]
                        n = step(dve.tensor_scalar(hot[:, t, j, :], iota[:, :], ridf[:, t, j:j + 1], w, ALU.is_equal, ALU.mult))
                after(n)
                if b >= 1:
                    full(dve, ("cT", b - 1))
                dve.tensor_copy(comb[:, :, NE], rw[:, :, 1]).then_inc(comb_done, 1)
                dve.tensor_tensor(comb[:, :, 0:NE], hot[:, :, 0, :], hot[:, :, 1, :], ALU.add).then_inc(comb_done, 1)

            quantize(0)
            adjacency(0)
            adjacency_sum(0)
            row_maxima(0, 0, NSF)
            split_maxima(0)
            for b in range(B + 1):
                nxt = b + 1 < B
                if nxt:
                    quantize(b + 1)
                    topk_rounds(b + 1, 0, ROUNDS // 2)
                if b < B:
                    attention_out(b)
                if b == 0:
                    row_maxima(1, 0, NSF)
                    topk_rounds(1, ROUNDS // 2, ROUNDS)
                else:
                    for f in range(NP2):
                        if nxt:
                            row_maxima(b + 1, NSF * f // NP2, NSF * (f + 1) // NP2)
                        hidden(b - 1, f)
                        if nxt:
                            topk_rounds(b + 1, ROUNDS // 2 + f, min(ROUNDS // 2 + f + 1, ROUNDS))
                if nxt:
                    split_maxima(b + 1)
                    adjacency(b + 1)
                if b > 0:
                    experts_out(b - 1)
                if nxt:
                    adjacency_sum(b + 1)
                if b < B:
                    router(b)

        @block.tensor
        def _(pe):
            def transposes(key, pieces):
                dst = begin_fill(pe, key)
                for put, src in pieces:
                    ins = pe.transpose(put(dst), src, ident[0:src.shape[0], 0:src.shape[0]])
                end_fill(ins, key)

            pe.wait_ge(consts, 3)
            pe.wait_ge(ld_wc, 32)
            transposes(("cw",), [(lambda d, k=k: d[0:D, k * D:(k + 1) * D], wc_sb[:, k, :]) for k in range(2)])
            pe.wait_ge(ld_ctx, 16)
            for hf in range(2):
                transposes(("ct", hf), [(lambda d, j=j: d[0:D, j * P:(j + 1) * P], ctx_sb[:, 4 * hf + j, :]) for j in range(4)])
            read_out(pe, ("cw",))
            for kind in range(2):
                for hf in range(2):
                    read_out(pe, ("ct", hf))
                    dst = begin_fill(pe, ("cq", kind, hf))
                    end_fill(pe.matmul(dst[:, :], wcT[:, kind, :], ctxT[:, hf * 512:(hf + 1) * 512], start=True, stop=True), ("cq", kind, hf))
            for b in range(B):
                read_out(pe, ("cq", 1, b // 2))
                read_out(pe, ("cq", 0, b // 2))
                dst = begin_fill(pe, ("sim", b))
                for t in range(QT):
                    tok = (QT * b + t) * P
                    ins = pe.matmul(dst[:, t * S:(t + 1) * S], qkcT[:, 0, tok:tok + P], qkcT[:, 1, b * S:(b + 1) * S], start=True, stop=True)
                end_fill(ins, ("sim", b))

            for n in range(4):
                pe.wait_ge(ld_x[n // 2], 16)
                transposes(("xt", n), [(lambda d, j=j: d[:, j * P:(j + 1) * P],
                                        x_sb[:, 4 * (n // 2) + j, (n % 2) * P:(n % 2 + 1) * P]) for j in range(4)])
            pe.wait_ge(ld_wqkv, 16)
            for n in range(8):
                hf, kind, g = n // 4, (n // 2) % 2, n % 2
                for k in range(KC):
                    read_out(pe, ("xt", 2 * hf + k))
                dst = begin_fill(pe, ("qk", n))
                for k in range(KC):
                    ins = pe.matmul(dst[:, :], wqkv[:, k, kind * C + g * P:kind * C + (g + 1) * P],
                                    xT[:, k, hf * 512:(hf + 1) * 512], start=(k == 0), stop=(k == KC - 1))
                end_fill(ins, ("qk", n))
            for n in range(4):
                dst = begin_fill(pe, ("v", n))
                for i in range(2):
                    tok = (2 * n + i) * P
                    for k in range(KC):
                        ins = pe.matmul(dst[:, i * C:(i + 1) * C], xT[:, k, tok:tok + P], wqkv[:, k, 2 * C:3 * C],
                                        start=(k == 0), stop=(k == KC - 1))
                end_fill(ins, ("v", n))
            pe.wait_ge(amax_done, 1)
            dst = begin_fill(pe, ("mx", 0))
            end_fill(pe.transpose(dst[0:3, 0:P], amax3[:, :], ident[:, :]), ("mx", 0))
            pe.wait_ge(gmax_done, 1)
            pe.wait_ge(consts, 7)
            dst = begin_fill(pe, ("mx", 1))
            end_fill(pe.matmul(dst[:, 0:3], ones[0:3, :], gdiag[:, :], start=True, stop=True), ("mx", 1))

            pe.wait_ge(ld_wg, 32)
            for n in range(NWT):
                which, pieces = n // (NWT // 3), []
                if which == 1:
                    pe.wait_ge(ld_wu, 32)
                if which == 2:
                    pe.wait_ge(ld_wd, 64)
                for j in range(4):
                    s = 4 * (n % (NWT // 3)) + j
                    if which < 2:
                        src = (wg_nat, wu_nat)[which][:, s % NF, (s // NF) * P:(s // NF + 1) * P]
                    else:
                        src = wd_nat[:, s % KC, s // KC, :]
                    pieces.append((lambda d, j=j: d[:, j * P:(j + 1) * P], src))
                transposes(("wt", n), pieces)
            pe.wait_ge(ld_gw, 32)
            transposes(("gw",), [(lambda d, k=k: d[:, k * 16:k * 16 + NW], gw_nat[:, k * P:(k + 1) * P]) for k in range(KC)])

            def adjacency_transposes(b):
                pe.wait_ge(adj_done, QT * (b + 1))
                transposes(("at", b), [(lambda d, i=i, j=j: d[:, i * S + j * P:i * S + (j + 1) * P], adj[:, j, i * P:(i + 1) * P])
                                       for i in range(QT) for j in range(QT)])

            def query_scores(b, first, last):
                if first == 0:
                    pe.wait_ge(q8_done, b + 1)
                    pe.wait_ge(km_done, NH * (b + 1))
                for i in range(first, last):
                    g, t, hp = i // (2 * HG // 2), (i // (HG // 2)) % 2, i % (HG // 2)
                    h = g * HG + 2 * hp
                    dst = begin_fill(pe, ("s", b, i))
                    end_fill(pe.matmul(dst[:, :], q8[:, b % 2, g, t * P:(t + 1) * P], kmask[:, b % 2, h:h + 2, :],
                                       start=True, stop=True), ("s", b, i))

            def maxima_across(b):
                pe.wait_ge(mparts_done, 2 * (b + 1))
                pe.wait_ge(consts, 9)
                dst = begin_fill(pe, ("mT", b))
                for t in range(QT):
                    ins = pe.transpose(dst[:, t * P // 2:(t + 1) * P // 2].bitcast(BF16), mparts[:, t, :], identb[:, :])
                end_fill(ins, ("mT", b))

            def key_scores(b, h):
                dst = begin_fill(pe, ("st", b, h))
                for t in range(QT):
                    pe.matmul(dst[:, t * S:(t + 1) * S], kmask[:, b % 2, h, t * P:(t + 1) * P], q8[:, b % 2, h // HG, :],
                              start=True, stop=False)
                    ins = pe.matmul(dst[:, t * S:(t + 1) * S], sel[:, h, :], mT[:, b % 2, :], start=False, stop=True)
                end_fill(ins, ("st", b, h))

            def attend(b, grp):
                key = ("av", b, grp // 2)
                dst = begin_fill(pe, key) if grp % 2 == 0 else bank[place[key][0]]
                if grp == 0:
                    pe.wait_ge(v_step, 3 * (b + 1))
                for h in range(4 * grp + 2, 4 * grp + 4):
                    read_out(pe, ("st", b, h))
                for t in range(QT):
                    for j in range(4):
                        h = 4 * grp + j
                        ins = pe.matmul(dst[SLOT * j:SLOT * (j + 1), (grp % 2) * S:(grp % 2 + 1) * S], v8[:, b % 2, t, h, :],
                                        expo[:, h % ER, t, :], start=(t == 0), stop=(t == QT - 1))
                if grp % 2:
                    end_fill(ins, key)
                else:
                    ins.then_inc(av_half, 1)

            def attention_out(b):
                for i in range(2):
                    read_out(pe, ("av", b, i))
                for t in range(QT):
                    transposes(("avt", b, t), [(lambda d, g=g: d[:, g * P:(g + 1) * P], avT[:, g, t * P:(t + 1) * P])
                                               for g in range(NG)])
                for t in range(QT):
                    read_out(pe, ("avt", b, t))
                transposes(("aT", b), [(lambda d, k=k, t=t: d[:, k * S + t * P:k * S + (t + 1) * P], attn[:, t, k * P:(k + 1) * P])
                                       for k in range(KC) for t in range(QT)])
                read_out(pe, ("aT", b))
                pe.wait_ge(ld_wout, 16)
                dst = begin_fill(pe, ("op", b))
                for t in range(QT):
                    for k in range(KC):
                        ins = pe.matmul(dst[:, t * C:(t + 1) * C], aT[:, k, t * P:(t + 1) * P], wout[:, k, :],
                                        start=(k == 0), stop=(k == KC - 1))
                end_fill(ins, ("op", b))

            def experts_in(b, f, name, w):
                dst = begin_fill(pe, (name, b, f))
                for i in range(2):
                    for k in range(KC):
                        ins = pe.matmul(dst[:, i * S:(i + 1) * S], w[:, k, 2 * f + i, :], x2T[:, b % 2, k, :],
                                        start=(k == 0), stop=(k == KC - 1))
                end_fill(ins, (name, b, f))

            def experts_out(b):
                dst = begin_fill(pe, ("y", b))
                for t in range(QT):
                    for f in range(NF):
                        if t == 0 and f % 2 == 0:
                            pe.wait_ge(hid_done, NP2 * b + f // 2 + 1)
                        ins = pe.matmul(dst[:, t * C:(t + 1) * C], hid[:, f, t * P:(t + 1) * P], wdT[:, f, :],
                                        start=(f == 0), stop=(f == NF - 1))
                end_fill(ins, ("y", b))

            def router(b):
                pe.wait_ge(x2_done, QT * (b + 1))
                transposes(("x2t", b), [(lambda d, k=k, t=t: d[:, k * S + t * P:k * S + (t + 1) * P], x2[:, b % 2, t, k * P:(k + 1) * P])
                                        for k in range(KC) for t in range(QT)])
                read_out(pe, ("x2t", b))
                dst = begin_fill(pe, ("rt", b))
                for t in range(QT):
                    for k in range(KC):
                        ins = pe.matmul(dst[:, t * 16:t * 16 + NW], x2T[:, b % 2, k, t * P:(t + 1) * P], gwT[:, k, :],
                                        start=(k == 0), stop=(k == KC - 1))
                end_fill(ins, ("rt", b))
                pe.wait_ge(comb_done, 2 * (b + 1))
                transposes(("cT", b), [(lambda d, t=t: d[0:NW, t * P:(t + 1) * P], comb[:, t, :]) for t in range(QT)])

            adjacency_transposes(0)
            query_scores(0, 0, NSF)
            maxima_across(0)
            for n in range(NWT):
                read_out(pe, ("wt", n))
            read_out(pe, ("gw",))
            for b in range(B + 1):
                nxt = b + 1 < B
                if b < B:
                    read_out(pe, ("mT", b))
                    for grp in range(NG + 1):
                        if grp < NG:
                            for j in range(4):
                                key_scores(b, 4 * grp + j)
                        if grp > 0:
                            attend(b, grp - 1)
                    attention_out(b)
                if b == 0:
                    query_scores(1, 0, NSF)
                    maxima_across(1)
                else:
                    for f in range(NP2):
                        experts_in(b - 1, f, "g", wgT)
                        if nxt:
                            query_scores(b + 1, NSF * f // NP2, NSF * (f + 1) // NP2)
                        experts_in(b - 1, f, "u", wuT)
                    if nxt:
                        maxima_across(b + 1)
                    experts_out(b - 1)
                if nxt:
                    adjacency_transposes(b + 1)
                if b < B:
                    router(b)


_INS = ['x', 'ctx_512', 'L0_attn_W_qkv', 'L0_attn_W_out', 'L0_attn_b_out', 'L0_xattn_Wq', 'L0_xattn_Wk',
        'L0_xattn_gamma_raw', 'L0_ffn_gate_w', 'L0_ffn_w_gate', 'L0_ffn_w_up', 'L0_ffn_w_down',
        'L0_ffn_sh_gate', 'L0_ffn_sh_up', 'L0_ffn_sh_down', 'L0_ffn_se_gate_w']
_OUTS = [((4, 256, 256), 'float32')]


def kernel(**inputs):
    import numpy as _np
    import concourse.bacc as _bacc
    from concourse import mybir as _mybir
    from concourse.bass_utils import run_bass_kernel_spmd as _run

    nc = _bacc.Bacc("TRN2", target_bir_lowering=False, num_devices=1)
    arrays, args = {}, []
    for name in _INS:
        a = _np.ascontiguousarray(inputs[name])
        arrays[f"in_{name}_dram"] = a
        args.append(nc.dram_tensor(f"in_{name}_dram", a.shape, _mybir.dt.from_np(a.dtype), kind="ExternalInput").ap())
    for i, (shape, dtype) in enumerate(_OUTS):
        dt = _mybir.dt.from_np(_np.dtype(dtype))
        args.append(nc.dram_tensor(f"out_{i}_dram", shape, dt, kind="ExternalOutput").ap())
    decoder_layer(nc, *args)
    r = _run(nc, [arrays], core_ids=[0])
    return r.results[0]["out_0_dram"]
```

```python
from contextlib import ExitStack

import concourse.bass as bass
from concourse import mybir

F32 = mybir.dt.float32
BF16 = mybir.dt.bfloat16
I32 = mybir.dt.int32
U32 = mybir.dt.uint32
ALU = mybir.AluOpType
ACT = mybir.ActivationFunctionType
AX = mybir.AxisListType

P = 128
FP8_MAX = 448.0
LN_EPS = 1e-5
TOP_K_RATIO = 0.3
E4M3_LEAST_NORMAL = 2.0 ** -6
E4M3_ROUNDER = 1.5 * 2.0 ** 20
EXPONENT_BITS = 0x7F800000
LOWEST = -3.0e38


def decoder_layer(nc, x, ctx_512, W_qkv, W_out, b_out, Wq, Wk, gamma_raw, gate_w, w_gate, w_up, w_down,
                  sh_gate, sh_up, sh_down, se_gate_w, out):
    B, S, C = x.shape
    TOK = B * S
    NT = TOK // P
    QT = S // P
    KC = C // P
    NH = 16
    HD = C // NH
    HG = P // HD
    D = ctx_512.shape[2]
    SIM_HEADS = 4
    SIM_SCALE = 1.0 / ((D // SIM_HEADS) ** 0.5 * SIM_HEADS)
    TOPK = max(1, int(S * TOP_K_RATIO))
    ROUNDS = (TOPK + 7) // 8
    NE, HM, _ = w_gate.shape
    HS = sh_gate.shape[0]
    NS = HS // P
    NF = NE + NS
    NW = NE + 1
    SLOT = 32
    NG = NH // 4
    ER = 8
    NSF = KC * QT * HG // 2
    assert HM == P and QT == 2 and KC == 2 and D == 64

    es = ExitStack()
    with es:
        def sb(name, shape, dt=F32):
            return es.enter_context(nc.sbuf_tensor(name, shape, dt))

        def sem(name):
            return es.enter_context(nc.semaphore(name))

        x_sb = sb("x_sb", [P, NT, C])
        ctx_sb = sb("ctx_sb", [P, NT, D])
        wc_sb = sb("wc_sb", [D, 2, D])
        place_qkv = sb("wqkv_avT_attn", [P, 3 * KC * C])
        wqkv = place_qkv[:].rearrange("p (k f) -> p k f", k=KC)
        wout = sb("wout", [P, KC, C])
        bout = sb("bout", [P, C])
        place_gu = sb("wgu_expo_silu", [P, 2 * NF * C])
        wg_nat = place_gu[:, 0:NF * C].rearrange("p (f c) -> p f c", f=NF)
        wu_nat = place_gu[:, NF * C:2 * NF * C].rearrange("p (f c) -> p f c", f=NF)
        place_d = sb("wd_hid", [P, NF * C])
        wd_nat = place_d[:].rearrange("p (k f h) -> p k f h", k=KC, f=NF)
        gw_nat = sb("gw_nat", [NW, C])
        graw = sb("graw", [P, 1])

        ident = sb("ident", [P, P])
        identb = sb("identb", [P, P], BF16)
        ones = sb("ones", [P, P])
        headmask = sb("headmask", [P, HG])
        sel = sb("sel", [P, NH, P], BF16)
        iota = sb("iota", [P, NE])
        halfneg = sb("halfneg", [P, QT])
        wcT = sb("wcT", [P, 2, P])
        place_t = sb("xT_ctxT_qkcT_wgT_wuT", [P, 5 * TOK])
        xT = place_t[:, 0:KC * TOK].rearrange("p (k s) -> p k s", k=KC)
        ctxT = place_t[:, KC * TOK:(KC + 1) * TOK]
        qkcT = place_t[:, (KC + 1) * TOK:(KC + 3) * TOK].rearrange("p (k s) -> p k s", k=2)
        sim = sb("sim", [P, NT, S])
        work = sb("work", [P, QT, S])
        top8 = sb("top8", [P, QT, 8])
        sig = sb("sig", [P, QT, S])
        adj = sb("adj", [P, QT, S])
        adjs = sb("adjs", [P, QT, S])
        gam = sb("gam", [P, 5])

        qkraw = sb("qkraw", [P, 2, KC, TOK])
        vraw = sb("vraw", [P, NT, C])
        amax = sb("amax", [P, 3, 4])
        amax3 = sb("amax3", [P, 3])
        gmax = sb("gmax", [2, 1])
        gmaxv = sb("gmaxv", [1, 1])
        gdiag = sb("gdiag", [2, 2])
        scale3 = sb("scale3", [P, 3])
        inv3 = sb("inv3", [P, 3])
        cexp = sb("cexp", [P, 1])

        qs = sb("qs", [P, 3, 2 * S])
        qm = sb("qm", [P, 3, 2 * S])
        k8 = sb("k8", [P, KC, S], BF16)
        q8 = sb("q8", [P, 2, KC, S], BF16)
        kmask = sb("kmask", [P, 2, NH, S], BF16)
        v8 = sb("v8", [P, 2, QT, NH, SLOT])
        negm = sb("negm", [P, QT, NH])
        mparts = sb("mparts", [P, QT, P], BF16)
        mT = sb("mT", [P, 2, S], BF16)
        expo = place_gu[:, 0:ER * QT * S].rearrange("p (h t s) -> p h t s", h=ER, t=QT)
        avT = place_qkv[:, 0:NG * S].rearrange("p (g s) -> p g s", g=NG)
        rsum = sb("rsum", [P, QT, NH])
        attn = place_qkv[:, NG * S:NG * S + QT * C].rearrange("p (t c) -> p t c", t=QT)
        aT = sb("aT", [P, KC, S])
        pre1 = sb("pre1", [P, QT, C])
        pre2 = sb("pre2", [P, QT, C])
        x2 = sb("x2", [P, 2, QT, C])
        yo = sb("yo", [P, 2, QT, C])
        stats = sb("stats", [P, 3, QT, 6])
        mv = sb("mv", [P, 3, QT, 2])
        vare = sb("vare", [P, 3, QT])
        rstd = sb("rstd", [P, 3, QT])
        rg = sb("rg", [P, QT])

        wgT = place_t[:, 0:KC * NF * P].rearrange("p (k f h) -> p k f h", k=KC, f=NF)
        wuT = place_t[:, KC * NF * P:2 * KC * NF * P].rearrange("p (k f h) -> p k f h", k=KC, f=NF)
        wdT = sb("wdT", [P, NF, C])
        gwT = sb("gwT", [P, KC, NW])
        x2T = sb("x2T", [P, 2, KC, S])
        rsc = sb("rsc", [P, QT, NW])
        rtop = sb("rtop", [P, QT, 8])
        ridx = sb("ridx", [P, QT, 8], U32)
        ridf = sb("ridf", [P, QT, 2])
        rarg = sb("rarg", [P, QT, 2])
        rtanh = sb("rtanh", [P, QT, 2])
        rw = sb("rw", [P, QT, 2])
        rw2 = sb("rw2", [P, QT, 1])
        hot = sb("hot", [P, QT, 2, NE])
        comb = sb("comb", [P, QT, NW])
        combT = sb("combT", [NW, S])
        cb = sb("cb", [P, NW, S])
        silu = place_gu[:, ER * QT * S:ER * QT * S + 4 * S].rearrange("p (n f s) -> p n f s", n=2, f=2)
        hid1 = sb("hid1", [P, 2, 2, S])
        hid = place_d[:].rearrange("p (f s) -> p f s", f=NF)
        comb_dram = nc.dram_tensor("comb_dram", (B, NW, S), F32, kind="Internal").ap()

        bank = {n: es.enter_context(nc.psum_tensor(n, [P, 512], F32))
                for n in ("SA0", "SA1", "ST0", "ST1", "AV0", "AV1", "MG", "MU")}

        filled = {n: sem("filled_" + n) for n in bank}
        emptied = {n: sem("emptied_" + n) for n in bank}
        place, count = {}, {n: 0 for n in bank}

        def plan(key, name):
            place[key] = (name, count[name])
            count[name] += 1

        four = ("AV0", "AV1", "MG", "MU")
        plan(("cw",), "SA0")
        for hf in range(2):
            plan(("ct", hf), ("SA1", "ST0")[hf])
        for kind in range(2):
            for hf in range(2):
                plan(("cq", kind, hf), ("SA0", "ST1")[hf])
        for b in range(B):
            plan(("sim", b), ("SA1", "ST0")[b % 2])
        for n in range(4):
            plan(("xt", n), four[n])
        for n in range(8):
            plan(("qk", n), four[n % 4])
        for n in range(4):
            plan(("v", n), four[n])
        for n in range(4):
            plan(("mx", n), "ST1")
        NWT = 3 * KC * NF // 4
        NWG = 2 * KC * NF // 4
        for n in range(NWG):
            plan(("wt", n), four[n % 4])
        for b in range(B):
            for i in range(NSF):
                plan(("s", b, i), ("SA0", "SA1")[i % 2])
            plan(("mT", b), "SA0")
            for h in range(NH):
                plan(("st", b, h), ("ST0", "ST1")[h % 2])
        for b in range(B + 1):
            if b < B:
                plan(("av", b, 0), "AV0")
                plan(("avt", b, 0), "AV0")
                plan(("aT", b), "AV0")
                plan(("at", b), "AV0")
                plan(("x2t", b), "AV0")
                plan(("av", b, 1), "AV1")
                plan(("avt", b, 1), "AV1")
                plan(("op", b), "AV1")
                plan(("rt", b), "AV1")
                plan(("cT", b), "AV1")
            if b == 0:
                plan(("gw",), "MG")
                for n in range(NWG, NWT):
                    plan(("wt", n), ("MU", "MG")[n % 2])
            else:
                for f in range(NF // 2):
                    plan(("g", b - 1, f), "MG")
                    plan(("u", b - 1, f), "MU")
                plan(("y", b - 1), "MG")

        def begin_fill(pe, key):
            name, n = place[key]
            if n:
                pe.wait_ge(emptied[name], n)
            return bank[name]

        def end_fill(ins, key):
            ins.then_inc(filled[place[key][0]], 1)

        def full(eng, key):
            name, n = place[key]
            eng.wait_ge(filled[name], n + 1)
            return bank[name]

        def release(ins, key):
            ins.then_inc(emptied[place[key][0]], 1)

        def read_out(eng, key):
            name, n = place[key]
            eng.wait_ge(emptied[name], n + 1)

        ld_ctx, ld_wc, ld_wqkv, ld_small = sem("ld_ctx"), sem("ld_wc"), sem("ld_wqkv"), sem("ld_small")
        ld_x = [sem(f"ld_x{i}") for i in range(2)]
        ld_wg, ld_wu, ld_wd, ld_gw, ld_wout = sem("ld_wg"), sem("ld_wu"), sem("ld_wd"), sem("ld_gw"), sem("ld_wout")
        const_step, consts = sem("const_step"), sem("consts")
        bias_added = sem("bias_added")
        gate_exp = sem("gamma_exp")
        tanh_done, topk_step, adj_done = sem("tanh_done"), sem("topk_step"), sem("adj_done")
        amax_done, gmax_done = sem("amax_done"), sem("gmax_done")
        scales_done = sem("scales_done")
        scaled = [sem(f"scaled_{n}") for n in "qkv"]
        q8_done, k8_done, km_done, v_step = sem("q8_done"), sem("k8_done"), sem("kmask_done"), sem("v_step")
        mparts_done = sem("mparts_done")
        av_half = sem("av_half")
        attn_done = sem("attn_done")
        mv_s = [sem(f"mean_var{i}_done") for i in range(3)]
        ve_s = [sem(f"var_eps{i}_done") for i in range(3)]
        rstd_s = [sem(f"rstd{i}_done") for i in range(3)]
        x2_done = sem("x2_done")
        rarg_done, rtanh_done, comb_done = sem("router_arg_done"), sem("router_tanh_done"), sem("comb_done")
        comb_written, cb_done = sem("comb_written"), sem("cb_done")
        silu_done, hid_done = sem("silu_done"), sem("hid_done")
        yo_done, out_done = sem("yo_done"), [sem(f"out_done{i}") for i in range(2)]
        dve_step = sem("dve_step")

        NP2 = NF // 2
        block = es.enter_context(nc.Block())

        @block.sync
        def _(sp):
            sp.dma_start(ctx_sb[:], ctx_512.rearrange("b (t p) d -> p (b t) d", p=P)).then_inc(ld_ctx, 16)
            sp.dma_start(wc_sb[:, 0, :], Wq).then_inc(ld_wc, 16)
            sp.dma_start(wc_sb[:, 1, :], Wk).then_inc(ld_wc, 16)
            xv = x.rearrange("b (t p) c -> p (b t) c", p=P)
            sp.dma_start(x_sb[:, 0:NT // 2, :], xv[:, 0:NT // 2, :]).then_inc(ld_x[0], 16)
            sp.dma_start(wqkv[:], W_qkv.rearrange("(k p) f -> p k f", p=P)).then_inc(ld_wqkv, 16)
            sp.dma_start(x_sb[:, NT // 2:NT, :], xv[:, NT // 2:NT, :]).then_inc(ld_x[1], 16)
            sp.dma_start(graw[:], gamma_raw.rearrange("(a c) -> a c", a=1).broadcast_to((P, 1))).then_inc(ld_small, 16)
            sp.dma_start(bout[:], b_out.rearrange("(a c) -> a c", a=1).broadcast_to((P, C))).then_inc(ld_small, 16)
            sp.dma_start(wg_nat[:, 0:NE, :], w_gate.rearrange("e h c -> h e c")).then_inc(ld_wg, 16)
            sp.dma_start(wg_nat[:, NE:NF, :], sh_gate.rearrange("(s h) c -> h s c", h=P)).then_inc(ld_wg, 16)
            sp.dma_start(wu_nat[:, 0:NE, :], w_up.rearrange("e h c -> h e c")).then_inc(ld_wu, 16)
            sp.dma_start(wu_nat[:, NE:NF, :], sh_up.rearrange("(s h) c -> h s c", h=P)).then_inc(ld_wu, 16)
            for k in range(KC):
                sp.dma_start(wd_nat[:, k, 0:NE, :], w_down[:, k * P:(k + 1) * P, :].rearrange("e c h -> c e h")).then_inc(ld_wd, 16)
                sp.dma_start(wd_nat[:, k, NE:NF, :], sh_down[k * P:(k + 1) * P, :].rearrange("c (s h) -> c s h", h=P)).then_inc(ld_wd, 16)
            sp.dma_start(gw_nat[0:NE, :], gate_w).then_inc(ld_gw, 16)
            sp.dma_start(gw_nat[NE:NW, :], se_gate_w).then_inc(ld_gw, 16)
            sp.dma_start(wout[:], W_out.rearrange("(k p) o -> p k o", p=P)).then_inc(ld_wout, 16)
            for b in range(B + 1):
                if b < B:
                    read_out(sp, ("cT", b))
                    sp.dma_start(comb_dram[b], combT[:]).then_inc(comb_written, 16)
                    sp.wait_ge(comb_written, 16 * (b + 1))
                    if b >= 1:
                        sp.wait_ge(hid_done, NP2 * b)
                    sp.dma_start(cb[:, :, :], comb_dram[b:b + 1].broadcast_to((P, NW, S))).then_inc(cb_done, 16)
                if b >= 1:
                    sp.wait_ge(yo_done, QT * b)
                    sp.dma_start(out[b - 1].rearrange("(t p) c -> p t c", p=P), yo[:, (b - 1) % 2]).then_inc(out_done[(b - 1) % 2], 16)
            for i in range(2):
                sp.wait_ge(out_done[i], 16 * (B // 2))
            sp.wait_ge(cb_done, 16 * B)

        @block.gpsimd
        def _(pool):
            pool.memset(ident[:], 0.0).then_inc(const_step, 1)
            pool.memset(wcT[:], 0.0).then_inc(consts, 1)
            pool.memset(ctxT, 0.0).then_inc(consts, 1)
            pool.wait_ge(const_step, 1)
            pool.affine_select(out=ident[:], in_=ident[:], compare_op=ALU.not_equal, fill=1.0, base=0,
                               pattern=[[-1, P]], channel_multiplier=1).then_inc(consts, 1)
            pool.memset(identb[:], 0.0).then_inc(const_step, 1)
            pool.memset(headmask[:], 1.0).then_inc(const_step, 1)
            pool.memset(sel[:], 0.0).then_inc(const_step, 1)
            pool.wait_ge(const_step, 4)
            pool.affine_select(out=identb[:], in_=identb[:], compare_op=ALU.not_equal, fill=1.0, base=0,
                               pattern=[[-1, P]], channel_multiplier=1).then_inc(consts, 1)
            pool.affine_select(out=headmask[:], in_=headmask[:], compare_op=ALU.is_ge, fill=0.0, base=0,
                               pattern=[[-HD, HG]], channel_multiplier=1).then_inc(const_step, 1)
            pool.affine_select(out=sel[:], in_=sel[:], compare_op=ALU.not_equal, fill=1.0, base=0,
                               pattern=[[-1, NH], [0, P]], channel_multiplier=1).then_inc(const_step, 1)
            pool.wait_ge(const_step, 6)
            pool.affine_select(out=headmask[:], in_=headmask[:], compare_op=ALU.is_ge, fill=0.0, base=HD - 1,
                               pattern=[[HD, HG]], channel_multiplier=-1).then_inc(consts, 1)
            pool.affine_select(out=sel[:], in_=sel[:], compare_op=ALU.not_equal, fill=1.0, base=-NH,
                               pattern=[[-1, NH], [0, P]], channel_multiplier=1).then_inc(consts, 1)
            pool.memset(ones[:], 1.0).then_inc(consts, 1)
            pool.memset(v8[:], 1.0).then_inc(consts, 1)
            pool.memset(mparts[:], 0.0).then_inc(consts, 1)
            pool.memset(halfneg[:], -0.5).then_inc(const_step, 1)
            pool.wait_ge(consts, 9)
            pool.wait_ge(const_step, 7)

            def quantize(b):
                pool.wait_ge(v_step, 3 * b + 1)
                pool.tensor_tensor(qs[:, 2, :], qs[:, 2, :], qm[:, 2, :], ALU.add).then_inc(v_step, 1)
                pool.wait_ge(v_step, 3 * b + 2)
                if b >= 2:
                    full(pool, ("av", b - 2, 1))
                pool.tensor_tensor(v8[:, b % 2, :, :, 0:HD], qs[:, 2, :].rearrange("p (t h d) -> p t h d", t=QT, h=NH),
                                   qm[:, 2, :].rearrange("p (t h d) -> p t h d", t=QT, h=NH),
                                   ALU.subtract).then_inc(v_step, 1)

            def inv_std(i, n):
                pool.wait_ge(mv_s[i], QT * (n + 1))
                pool.tensor_scalar(vare[:, i, :], mv[:, i, :, 1], LN_EPS, None, ALU.add).then_inc(ve_s[i], 1)
                pool.wait_ge(ve_s[i], n + 1)
                pool.tensor_tensor(rstd[:, i, :], vare[:, i, :], halfneg[:], ALU.pow).then_inc(rstd_s[i], 1)

            def weigh_hidden(b, f):
                if f == 0:
                    pool.wait_ge(cb_done, 16 * (b + 1))
                    if b >= 1:
                        full(pool, ("y", b - 1))
                    else:
                        full(pool, ("wt", NWT - 1))
                n = b * NP2 + f
                read_out(pool, ("u", b, f))
                for i in range(2):
                    e = min(2 * f + i, NE)
                    ins = pool.tensor_tensor(hid[:, 2 * f + i, :], hid1[:, n % 2, i, :], cb[:, e, :], ALU.mult)
                ins.then_inc(hid_done, 1)

            quantize(0)
            pool.wait_ge(ld_small, 32)
            for n in range(4):
                full(pool, ("xt", n))
            for t in range(NT):
                pool.tensor_tensor(x_sb[:, t, :], x_sb[:, t, :], bout[:], ALU.add).then_inc(bias_added, 1)
            for b in range(B + 1):
                if b + 1 < B:
                    quantize(b + 1)
                if b > 0:
                    weigh_hidden(b - 1, 0)
                if b < B:
                    inv_std(0, b)
                    inv_std(1, b)
                if b > 0:
                    for f in range(1, NP2):
                        weigh_hidden(b - 1, f)
                    inv_std(2, b - 1)

        @block.scalar
        def _(act):
            act.wait_ge(consts, 2)
            src = full(act, ("cw",))
            release(act.copy(wcT[0:D, :, 0:D], src[0:D, 0:2 * D].rearrange("p (k d) -> p k d", k=2)), ("cw",))
            for hf in range(2):
                src = full(act, ("ct", hf))
                release(act.copy(ctxT[0:D, hf * 512:(hf + 1) * 512], src[0:D, :]), ("ct", hf))
            for kind in range(2):
                for hf in range(2):
                    src = full(act, ("cq", kind, hf))
                    release(act.copy(qkcT[:, kind, hf * 512:(hf + 1) * 512], src[:, :]), ("cq", kind, hf))
            for b in range(B):
                src = full(act, ("sim", b))
                release(act.mul(sim[:, QT * b:QT * (b + 1), :], src[:, :].rearrange("p (t s) -> p t s", t=QT), SIM_SCALE), ("sim", b))
            act.wait_ge(ld_small, 32)
            act.activation(gam[:, 0:1], graw[:, :], ACT.Exp, scale=-1.0).then_inc(gate_exp, 1)

            def tanh_sim(b):
                read_out(act, ("sim", b))
                if b >= 1:
                    act.wait_ge(adj_done, QT * b)
                act.activation(sig[:, :, :], sim[:, QT * b:QT * (b + 1), :], ACT.Tanh, scale=0.5).then_inc(tanh_done, 1)

            for n in (0, 2):
                src = full(act, ("xt", n))
                release(act.copy(xT[:, n % 2, (n // 2) * 512:(n // 2 + 1) * 512], src[:, :]), ("xt", n))
            tanh_sim(0)
            for n in range(8):
                hf, kind, g = n // 4, (n // 2) % 2, n % 2
                src = full(act, ("qk", n))
                release(act.copy(qkraw[:, kind, g, hf * 512:(hf + 1) * 512], src[:, :]), ("qk", n))
            def scale_qkv(b, kind):
                act.wait_ge(scales_done, 2 if kind < 2 else 3)
                if b >= 1:
                    act.wait_ge((q8_done, k8_done, v_step)[kind], b if kind < 2 else 3 * b)
                src = qkraw[:, kind, :, b * S:(b + 1) * S] if kind < 2 else vraw[:, QT * b:QT * (b + 1), :]
                act.activation(qs[:, kind, :].rearrange("p (t s) -> p t s", t=2), src, ACT.Copy,
                               scale=inv3[:, kind:kind + 1]).then_inc(scaled[kind], 1)

            def weights_out(n):
                src = full(act, ("wt", n))
                dst = (place_t[:, 0:KC * NF * P], place_t[:, KC * NF * P:2 * KC * NF * P],
                       wdT[:].rearrange("p f c -> p (f c)"))[n // (NWT // 3)]
                m = n % (NWT // 3)
                release(act.copy(dst[:, m * 512:(m + 1) * 512], src[:, :]), ("wt", n))

            def values_out(n):
                src = full(act, ("v", n))
                release(act.copy(vraw[:, 2 * n:2 * n + 2, :], src[:, :].rearrange("p (t c) -> p t c", t=2)), ("v", n))

            for n in range(4):
                values_out(n)
                if n in (1, 2):
                    scale_qkv(0, 2 - n)
            weights_out(0)
            weights_out(1)
            scale_qkv(0, 2)
            for n in range(2, NWG):
                weights_out(n)

            def spread_keys(b, first, last):
                if first == 0:
                    act.wait_ge(consts, 9)
                    act.wait_ge(k8_done, b + 1)
                    if b >= 2:
                        full(act, ("st", b - 2, NH - 1))
                for h in range(first, last):
                    act.activation(kmask[:, b % 2, h, :], k8[:, h // HG, :], ACT.Copy,
                                   scale=headmask[:, h % HG:h % HG + 1]).then_inc(km_done, 1)

            def exponentials(b):
                for h in range(NH):
                    src = full(act, ("st", b, h))
                    grp = (b * NH + h) // 4 - ER // 4
                    if grp >= 0 and grp % 2 == 0:
                        act.wait_ge(av_half, grp // 2 + 1)
                    elif grp >= 0:
                        full(act, ("av", grp // NG, grp % NG // 2))
                    release(act.activation(expo[:, h % ER, :, :], src[:, :].rearrange("p (t s) -> p t s", t=QT), ACT.Exp,
                                           scale=cexp[:, 0:1]), ("st", b, h))
                    if h == NH // 2 + 3:
                        attended(b, 0)
                attended(b, 1)

            def attended(b, i):
                src = full(act, ("av", b, i))
                if b >= 1 and i == 0:
                    full(act, ("avt", b - 1, QT - 1))
                release(act.copy(avT[:, 2 * i:2 * i + 2, :], src[:, :].rearrange("p (g s) -> p g s", g=2)), ("av", b, i))

            def silus(b, f):
                n = b * NP2 + f
                src = full(act, ("g", b, f))
                if n >= 2:
                    read_out(act, ("u", (n - 2) // NP2, (n - 2) % NP2))
                release(act.activation(silu[:, n % 2, :, :], src[:, :].rearrange("p (f s) -> p f s", f=2),
                                       ACT.Silu), ("g", b, f))

            for b in range(B + 1):
                nxt = b + 1 < B
                if nxt:
                    for kind in (1, 0, 2):
                        scale_qkv(b + 1, kind)
                if b < B:
                    exponentials(b)
                if b == 0:
                    src = full(act, ("gw",))
                    release(act.copy(gwT[:, :, :], src[:, 0:KC * 16].rearrange("p (k n) -> p k n", k=KC)[:, :, 0:NW]), ("gw",))
                if nxt:
                    tanh_sim(b + 1)
                    spread_keys(b + 1, 0, NH // 4)
                if b > 0:
                    silus(b - 1, 0)
                if b < B:
                    src = full(act, ("aT", b))
                    if b >= 1:
                        full(act, ("op", b - 1))
                    release(act.copy(aT[:, :, :], src[:, :].rearrange("p (k s) -> p k s", k=KC)), ("aT", b))
                if b > 0:
                    silus(b - 1, 1)
                if nxt:
                    spread_keys(b + 1, NH // 4, NH)
                if b == 0:
                    for n in range(NWG, NWT):
                        weights_out(n)
                else:
                    silus(b - 1, 2)
                    silus(b - 1, 3)
                if b < B:
                    src = full(act, ("x2t", b))
                    release(act.copy(x2T[:, b % 2, :, :], src[:, :].rearrange("p (k s) -> p k s", k=KC)), ("x2t", b))
                if b > 0:
                    silus(b - 1, 4)
                if b < B:
                    act.wait_ge(rarg_done, 2 * (b + 1))
                    act.activation(rtanh[:, :, :], rarg[:, :, :], ACT.Tanh, scale=0.5).then_inc(rtanh_done, 1)
                    src = full(act, ("cT", b))
                    if b >= 1:
                        act.wait_ge(comb_written, 16 * b)
                    release(act.copy(combT[:, :], src[0:NW, 0:S]), ("cT", b))

        @block.vector
        def _(dve):
            steps = [0]

            def step(ins):
                ins.then_inc(dve_step, 1)
                steps[0] += 1
                return steps[0]

            def after(n):
                dve.wait_ge(dve_step, n)

            for e in range(NE):
                dve.memset(iota[:, e:e + 1], float(e))

            def topk_rounds(b, first, last):
                base = b * (4 * ROUNDS - 2)
                if first == 0:
                    read_out(dve, ("sim", b))
                for r in range(first, last):
                    for t in range(QT):
                        if r > 0:
                            dve.wait_ge(topk_step, base + 4 * (r - 1) + 3 + t)
                        src = work[:, t, :] if r else sim[:, QT * b + t, :]
                        dve.max(top8[:, t, :], src).then_inc(topk_step, 1)
                    if r + 1 < ROUNDS:
                        for t in range(QT):
                            dve.wait_ge(topk_step, base + 4 * r + 1 + t)
                            src = work[:, t, :] if r else sim[:, QT * b + t, :]
                            dve.match_replace(work[:, t, :], top8[:, t, :], src, LOWEST).then_inc(topk_step, 1)

            def adjacency(b):
                dve.wait_ge(tanh_done, b + 1)
                after(gamma_step)
                n = step(dve.tensor_scalar(sig[:, :, :], sig[:, :, :], gam[:, 3:4], gam[:, 3:4], ALU.mult, ALU.add))
                dve.wait_ge(topk_step, (b + 1) * (4 * ROUNDS - 2))
                after(n)
                least = (TOPK - 1) % 8
                for t in range(QT):
                    dve.scalar_tensor_tensor(out=adj[:, t, :], in0=sim[:, QT * b + t, :], scalar=top8[:, t, least:least + 1],
                                             in1=sig[:, t, :], op0=ALU.is_ge, op1=ALU.mult).then_inc(adj_done, 1)

            def adjacency_sum(b):
                src = full(dve, ("at", b))
                release(dve.tensor_tensor(adjs[:, :, :], src[:, :].rearrange("p (t s) -> p t s", t=QT),
                                          adj[:, :, :], ALU.add), ("at", b))

            dve.wait_ge(gate_exp, 1)
            n = step(dve.tensor_scalar(gam[:, 1:2], gam[:, 0:1], 1.0, None, ALU.add))
            after(n)
            n = step(dve.reciprocal(gam[:, 2:3], gam[:, 1:2]))
            after(n)
            step(dve.tensor_scalar(gam[:, 3:4], gam[:, 2:3], 0.25, None, ALU.mult))
            gamma_step = step(dve.tensor_scalar(gam[:, 4:5], gam[:, 2:3], -1.0, 2.0, ALU.mult, ALU.add))

            for n in (1, 3):
                src = full(dve, ("xt", n))
                release(dve.tensor_copy(xT[:, n % 2, (n // 2) * 512:(n // 2 + 1) * 512], src[:, :]), ("xt", n))

            def abs_max(kind, j, key, src):
                read_out(dve, key)
                return step(dve.tensor_reduce(amax[:, kind, j:j + 1], src, AX.X, ALU.max, apply_absolute_value=True))

            def quantize(b, kind):
                dve.wait_ge(scaled[kind], b + 1)
                if b >= 1 and kind == 2:
                    dve.wait_ge(v_step, 3 * b)
                n = step(dve.tensor_scalar(qm[:, kind, :].bitcast(I32), qs[:, kind, :].bitcast(I32), EXPONENT_BITS, None,
                                           ALU.bitwise_and))
                after(n)
                rounder = dve.tensor_scalar(qm[:, kind, :], qm[:, kind, :], E4M3_LEAST_NORMAL, E4M3_ROUNDER,
                                            ALU.max, ALU.mult)
                if kind == 2:
                    rounder.then_inc(v_step, 1)
                    return
                after(step(rounder))
                n = step(dve.tensor_tensor(qs[:, kind, :], qs[:, kind, :], qm[:, kind, :], ALU.add))
                after(n)
                if kind == 0:
                    if b >= 2:
                        full(dve, ("st", b - 2, NH - 1))
                    dst, done = q8[:, b % 2], q8_done
                else:
                    if b >= 1:
                        dve.wait_ge(km_done, NH * b)
                    dst, done = k8[:, :, :], k8_done
                dve.tensor_tensor(dst, qs[:, kind, :].rearrange("p (k s) -> p k s", k=KC),
                                  qm[:, kind, :].rearrange("p (k s) -> p k s", k=KC), ALU.subtract).then_inc(done, 1)

            def spread_keys(b, first, last):
                dve.wait_ge(consts, 9)
                dve.wait_ge(k8_done, b + 1)
                for h in range(first, last):
                    dve.tensor_scalar(kmask[:, b % 2, h, :], k8[:, h // HG, :], headmask[:, h % HG:h % HG + 1], None,
                                      ALU.mult).then_inc(km_done, 1)

            def row_maxima(b, first, last):
                for i in range(first, last):
                    g, t, hp = i // (2 * HG // 2), (i // (HG // 2)) % 2, i % (HG // 2)
                    h = g * HG + 2 * hp
                    src = full(dve, ("s", b, i))
                    release(dve.tensor_reduce(negm[:, t, h:h + 2], src[:, :].rearrange("p (h s) -> p h s", h=2), AX.X,
                                              ALU.max, negate=True), ("s", b, i))

            def split_maxima(b):
                read_out(dve, ("s", b, NSF - 1))
                read_out(dve, ("s", b, NSF - 2))
                if b >= 1:
                    full(dve, ("mT", b - 1))
                dve.tensor_copy(mparts[:, :, 0:NH], negm[:, :, :]).then_inc(mparts_done, 1)
                dve.wait_ge(mparts_done, 2 * b + 1)
                dve.tensor_tensor(mparts[:, :, NH:2 * NH], negm[:, :, :], mparts[:, :, 0:NH], ALU.subtract).then_inc(mparts_done, 1)
                src = full(dve, ("mT", b))
                if b >= 2:
                    full(dve, ("st", b - 2, NH - 1))
                release(dve.tensor_copy(mT[:, b % 2, :], src[:, 0:S // 2].bitcast(BF16)), ("mT", b))

            def statistics(i, src):
                for t in range(QT):
                    n = step(dve.bn_stats(stats[:, i, t, :], src[:, t, :]))
                for t in range(QT):
                    after(n - QT + 1 + t)
                    dve.bn_aggr(mv[:, i, t, :], stats[:, i, t, :]).then_inc(mv_s[i], 1)

            def heads_out(b):
                for t in range(QT):
                    src = full(dve, ("avt", b, t))[:, :].rearrange("p (h s) -> p h s", h=NH)
                    n = step(dve.reciprocal(rsum[:, t, :], src[:, :, HD]))
                    after(n)
                    n = step(dve.tensor_scalar(rsum[:, t, :], rsum[:, t, :], scale3[:, 2:3], None, ALU.mult))
                    after(n)
                    if b >= 1 and t == 0:
                        full(dve, ("aT", b - 1))
                    release(dve.tensor_tensor(attn[:, t, :].rearrange("p (h d) -> p h d", h=NH), src[:, :, 0:HD],
                                              rsum[:, t, :].unsqueeze(2).broadcast_to((P, NH, HD)), ALU.mult), ("avt", b, t))

            def residual1(b):
                src = full(dve, ("op", b))
                dve.wait_ge(bias_added, NT)
                release(dve.tensor_tensor(pre1[:, :, :], src[:, :].rearrange("p (t c) -> p t c", t=QT),
                                          x_sb[:, QT * b:QT * (b + 1), :], ALU.add), ("op", b))
                read_out(dve, ("op", b))
                statistics(0, pre1)

            def residual2(b):
                dve.wait_ge(rstd_s[0], b + 1)
                n = step(dve.tensor_scalar(rg[:, :], rstd[:, 0, :], gam[:, 4:5], None, ALU.mult))
                after(n)
                for t in range(QT):
                    n = step(dve.tensor_scalar(pre1[:, t, :], pre1[:, t, :], mv[:, 0, t, 0:1], rg[:, t:t + 1],
                                               ALU.subtract, ALU.mult))
                after(n)
                n = step(dve.tensor_tensor(pre2[:, :, :], pre1[:, :, :], adjs[:, :, :], ALU.add))
                after(n)
                statistics(1, pre2)

            def norm2(b):
                dve.wait_ge(rstd_s[1], b + 1)
                for t in range(QT):
                    dve.tensor_scalar(x2[:, b % 2, t, :], pre2[:, t, :], mv[:, 1, t, 0:1], rstd[:, 1, t:t + 1],
                                      ALU.subtract, ALU.mult).then_inc(x2_done, 1)

            def hidden(b, f):
                n = b * NP2 + f
                dve.wait_ge(emptied["MG"], place[("g", b, f)][1] + 1)
                if n >= 2:
                    dve.wait_ge(hid_done, n - 1)
                src = full(dve, ("u", b, f))
                release(dve.tensor_tensor(hid1[:, n % 2, :, :], src[:, :].rearrange("p (f s) -> p f s", f=2),
                                          silu[:, n % 2, :, :], ALU.mult), ("u", b, f))

            def experts_out(b):
                src = full(dve, ("y", b))
                release(dve.tensor_tensor(pre1[:, :, :], src[:, :].rearrange("p (t c) -> p t c", t=QT),
                                          x2[:, b % 2], ALU.add), ("y", b))
                read_out(dve, ("y", b))
                statistics(2, pre1)
                dve.wait_ge(rstd_s[2], b + 1)
                if b >= 2:
                    dve.wait_ge(out_done[b % 2], 16 * (b // 2))
                for t in range(QT):
                    dve.tensor_scalar(yo[:, b % 2, t, :], pre1[:, t, :], mv[:, 2, t, 0:1], rstd[:, 2, t:t + 1],
                                      ALU.subtract, ALU.mult).then_inc(yo_done, 1)

            def router_scores(b):
                src = full(dve, ("rt", b))[:, 0:QT * 16].rearrange("p (t n) -> p t n", t=QT)
                release(dve.tensor_copy(rsc[:, :, :], src[:, :, 0:NW]), ("rt", b))
                read_out(dve, ("rt", b))
                for t in range(QT):
                    n = step(dve.max(rtop[:, t, :], rsc[:, t, 0:NE]))
                dve.tensor_copy(rarg[:, :, 1], rsc[:, :, NE]).then_inc(rarg_done, 1)
                after(n)
                dve.tensor_tensor(rarg[:, :, 0], rtop[:, :, 0], rtop[:, :, 1], ALU.subtract).then_inc(rarg_done, 1)
                for t in range(QT):
                    n = step(dve.max_index(ridx[:, t, :], rtop[:, t, :], rsc[:, t, 0:NE]))
                after(n)
                return step(dve.tensor_copy(ridf[:, :, :], ridx[:, :, 0:2]))

            def router_weights(b, found):
                dve.wait_ge(rtanh_done, b + 1)
                dve.tensor_scalar(rw[:, :, :], rtanh[:, :, :], 0.5, 0.5, ALU.mult, ALU.add)
                n = step(dve.tensor_scalar(rw2[:, :, 0], rtanh[:, :, 0], -0.5, 0.5, ALU.mult, ALU.add))
                after(found)
                after(n)
                for t in range(QT):
                    for j in range(2):
                        w = rw[:, t, 0:1] if j == 0 else rw2[:, t, 0:1]
                        n = step(dve.tensor_scalar(hot[:, t, j, :], iota[:, :], ridf[:, t, j:j + 1], w, ALU.is_equal, ALU.mult))
                after(n)
                if b >= 1:
                    full(dve, ("cT", b - 1))
                dve.tensor_copy(comb[:, :, NE], rw[:, :, 1]).then_inc(comb_done, 1)
                dve.tensor_tensor(comb[:, :, 0:NE], hot[:, :, 0, :], hot[:, :, 1, :], ALU.add).then_inc(comb_done, 1)

            for n in range(8):
                hf, kind, g = n // 4, (n // 2) % 2, n % 2
                topk_rounds(0, n, n + 1)
                m = abs_max(kind, 2 * hf + g, ("qk", n), qkraw[:, kind, g, hf * 512:(hf + 1) * 512])
            after(m)
            dve.tensor_reduce(amax3[:, 0:2], amax[:, 0:2, :], AX.X, ALU.max).then_inc(amax_done, 1)
            topk_rounds(0, 8, 9)
            src = full(dve, ("mx", 0))
            release(dve.tensor_reduce(gmax[:, :], src[0:2, 0:P], AX.X, ALU.max), ("mx", 0))
            read_out(dve, ("mx", 0))
            dve.tensor_scalar(gdiag[:, :], ident[0:2, 0:2], gmax[:, 0:1], None, ALU.mult).then_inc(gmax_done, 1)
            topk_rounds(0, 9, 10)
            src = full(dve, ("mx", 1))
            release(dve.tensor_scalar(scale3[:, 0:2], src[:, 0:2], 1.0 / FP8_MAX, None, ALU.mult), ("mx", 1))
            read_out(dve, ("mx", 1))
            dve.reciprocal(inv3[:, 0:2], scale3[:, 0:2]).then_inc(scales_done, 1)
            n = step(dve.tensor_scalar(cexp[:, :], scale3[:, 0:1], HD ** -0.5, None, ALU.mult))
            after(n)
            dve.tensor_scalar(cexp[:, :], cexp[:, :], scale3[:, 1:2], None, ALU.mult).then_inc(scales_done, 1)
            for n in range(4):
                m = abs_max(2, n, ("v", n), vraw[:, 2 * n:2 * n + 2, :].rearrange("p t c -> p (t c)"))
                if n == 1:
                    quantize(0, 1)
                if n == 2:
                    quantize(0, 0)
            after(m)
            dve.tensor_reduce(amax3[:, 2:3], amax[:, 2, :], AX.X, ALU.max).then_inc(amax_done, 1)
            spread_keys(0, 0, 8)
            src = full(dve, ("mx", 2))
            release(dve.tensor_reduce(gmaxv[:, :], src[0:1, 0:P], AX.X, ALU.max), ("mx", 2))
            spread_keys(0, 8, NH)
            src = full(dve, ("mx", 3))
            release(dve.tensor_scalar(scale3[:, 2:3], src[:, 0:1], 1.0 / FP8_MAX, None, ALU.mult), ("mx", 3))
            read_out(dve, ("mx", 3))
            dve.reciprocal(inv3[:, 2:3], scale3[:, 2:3]).then_inc(scales_done, 1)
            quantize(0, 2)
            adjacency(0)
            row_maxima(0, 0, NSF)
            split_maxima(0)

            HALF = ROUNDS // 2
            for b in range(B + 1):
                nxt, now, before = b + 1 < B, b < B, b > 0
                if nxt:
                    for kind in (1, 0, 2):
                        quantize(b + 1, kind)
                if now:
                    if before:
                        topk_rounds(b, HALF, ROUNDS)
                        adjacency(b)
                    heads_out(b)
                if before:
                    hidden(b - 1, 0)
                if nxt:
                    topk_rounds(b + 1, 0, 1)
                if now:
                    residual1(b)
                    adjacency_sum(b)
                    if nxt:
                        topk_rounds(b + 1, 1, 2)
                    residual2(b)
                if before:
                    hidden(b - 1, 1)
                if nxt:
                    row_maxima(b + 1, 0, 2)
                if now:
                    norm2(b)
                if nxt:
                    row_maxima(b + 1, 2, 4)
                if before:
                    hidden(b - 1, 2)
                if nxt:
                    row_maxima(b + 1, 4, 7)
                if before:
                    hidden(b - 1, 3)
                if nxt:
                    row_maxima(b + 1, 7, 13)
                if now:
                    found = router_scores(b)
                if before:
                    hidden(b - 1, 4)
                if nxt:
                    row_maxima(b + 1, 13, NSF)
                    split_maxima(b + 1)
                if now:
                    router_weights(b, found)
                if nxt:
                    topk_rounds(b + 1, 2, HALF)
                if before:
                    experts_out(b - 1)

        @block.tensor
        def _(pe):
            def transposes(key, pieces):
                dst = begin_fill(pe, key)
                for put, src in pieces:
                    ins = pe.transpose(put(dst), src, ident[0:src.shape[0], 0:src.shape[0]])
                end_fill(ins, key)

            pe.wait_ge(consts, 3)
            pe.wait_ge(ld_wc, 32)
            transposes(("cw",), [(lambda d, k=k: d[0:D, k * D:(k + 1) * D], wc_sb[:, k, :]) for k in range(2)])
            pe.wait_ge(ld_ctx, 16)
            for hf in range(2):
                transposes(("ct", hf), [(lambda d, j=j: d[0:D, j * P:(j + 1) * P], ctx_sb[:, 4 * hf + j, :]) for j in range(4)])
            read_out(pe, ("cw",))
            for kind in range(2):
                for hf in range(2):
                    read_out(pe, ("ct", hf))
                    dst = begin_fill(pe, ("cq", kind, hf))
                    end_fill(pe.matmul(dst[:, :], wcT[:, kind, :], ctxT[:, hf * 512:(hf + 1) * 512], start=True, stop=True), ("cq", kind, hf))
            for b in range(B):
                read_out(pe, ("cq", 1, b // 2))
                read_out(pe, ("cq", 0, b // 2))
                dst = begin_fill(pe, ("sim", b))
                for t in range(QT):
                    tok = (QT * b + t) * P
                    ins = pe.matmul(dst[:, t * S:(t + 1) * S], qkcT[:, 0, tok:tok + P], qkcT[:, 1, b * S:(b + 1) * S], start=True, stop=True)
                end_fill(ins, ("sim", b))

            for n in range(4):
                pe.wait_ge(ld_x[n // 2], 16)
                transposes(("xt", n), [(lambda d, j=j: d[:, j * P:(j + 1) * P],
                                        x_sb[:, 4 * (n // 2) + j, (n % 2) * P:(n % 2 + 1) * P]) for j in range(4)])
            pe.wait_ge(ld_wqkv, 16)
            for n in range(8):
                hf, kind, g = n // 4, (n // 2) % 2, n % 2
                for k in range(KC):
                    read_out(pe, ("xt", 2 * hf + k))
                dst = begin_fill(pe, ("qk", n))
                for k in range(KC):
                    ins = pe.matmul(dst[:, :], wqkv[:, k, kind * C + g * P:kind * C + (g + 1) * P],
                                    xT[:, k, hf * 512:(hf + 1) * 512], start=(k == 0), stop=(k == KC - 1))
                end_fill(ins, ("qk", n))
            def values(n):
                dst = begin_fill(pe, ("v", n))
                for i in range(2):
                    tok = (2 * n + i) * P
                    for k in range(KC):
                        ins = pe.matmul(dst[:, i * C:(i + 1) * C], xT[:, k, tok:tok + P], wqkv[:, k, 2 * C:3 * C],
                                        start=(k == 0), stop=(k == KC - 1))
                end_fill(ins, ("v", n))

            def weights_across(n):
                which, pieces = n // (NWT // 3), []
                if n % (NWT // 3) == 0:
                    pe.wait_ge((ld_wg, ld_wu, ld_wd)[which], 64 if which == 2 else 32)
                for j in range(4):
                    s = 4 * (n % (NWT // 3)) + j
                    if which < 2:
                        src = (wg_nat, wu_nat)[which][:, s % NF, (s // NF) * P:(s // NF + 1) * P]
                    else:
                        src = wd_nat[:, s % KC, s // KC, :]
                    pieces.append((lambda d, j=j: d[:, j * P:(j + 1) * P], src))
                transposes(("wt", n), pieces)

            values(0)
            pe.wait_ge(amax_done, 1)
            dst = begin_fill(pe, ("mx", 0))
            end_fill(pe.transpose(dst[0:2, 0:P], amax3[:, 0:2], ident[:, :]), ("mx", 0))
            values(1)
            pe.wait_ge(gmax_done, 1)
            pe.wait_ge(consts, 7)
            dst = begin_fill(pe, ("mx", 1))
            end_fill(pe.matmul(dst[:, 0:2], ones[0:2, :], gdiag[:, :], start=True, stop=True), ("mx", 1))
            values(2)
            values(3)
            weights_across(0)
            weights_across(1)
            pe.wait_ge(amax_done, 2)
            dst = begin_fill(pe, ("mx", 2))
            end_fill(pe.transpose(dst[0:1, 0:P], amax3[:, 2:3], ident[:, :]), ("mx", 2))
            weights_across(2)
            read_out(pe, ("mx", 2))
            dst = begin_fill(pe, ("mx", 3))
            end_fill(pe.matmul(dst[:, 0:1], ones[0:1, :], gmaxv[:, :], start=True, stop=True), ("mx", 3))
            for n in range(3, NWG):
                weights_across(n)

            def adjacency_transposes(b):
                pe.wait_ge(adj_done, QT * (b + 1))
                transposes(("at", b), [(lambda d, i=i, j=j: d[:, i * S + j * P:i * S + (j + 1) * P], adj[:, j, i * P:(i + 1) * P])
                                       for i in range(QT) for j in range(QT)])

            def query_scores(b, first, last):
                if first == 0:
                    pe.wait_ge(q8_done, b + 1)
                    pe.wait_ge(km_done, NH * (b + 1))
                for i in range(first, last):
                    g, t, hp = i // (2 * HG // 2), (i // (HG // 2)) % 2, i % (HG // 2)
                    h = g * HG + 2 * hp
                    dst = begin_fill(pe, ("s", b, i))
                    end_fill(pe.matmul(dst[:, :], q8[:, b % 2, g, t * P:(t + 1) * P], kmask[:, b % 2, h:h + 2, :],
                                       start=True, stop=True), ("s", b, i))

            def maxima_across(b):
                pe.wait_ge(mparts_done, 2 * (b + 1))
                pe.wait_ge(consts, 9)
                dst = begin_fill(pe, ("mT", b))
                for t in range(QT):
                    ins = pe.transpose(dst[:, t * P // 2:(t + 1) * P // 2].bitcast(BF16), mparts[:, t, :], identb[:, :])
                end_fill(ins, ("mT", b))

            def key_scores(b, h):
                dst = begin_fill(pe, ("st", b, h))
                for t in range(QT):
                    pe.matmul(dst[:, t * S:(t + 1) * S], kmask[:, b % 2, h, t * P:(t + 1) * P], q8[:, b % 2, h // HG, :],
                              start=True, stop=False)
                    ins = pe.matmul(dst[:, t * S:(t + 1) * S], sel[:, h, :], mT[:, b % 2, :], start=False, stop=True)
                end_fill(ins, ("st", b, h))

            def attend(b, grp):
                key = ("av", b, grp // 2)
                dst = begin_fill(pe, key) if grp % 2 == 0 else bank[place[key][0]]
                if grp == 0:
                    pe.wait_ge(v_step, 3 * (b + 1))
                for h in range(4 * grp + 2, 4 * grp + 4):
                    read_out(pe, ("st", b, h))
                for t in range(QT):
                    for j in range(4):
                        h = 4 * grp + j
                        ins = pe.matmul(dst[SLOT * j:SLOT * (j + 1), (grp % 2) * S:(grp % 2 + 1) * S], v8[:, b % 2, t, h, :],
                                        expo[:, h % ER, t, :], start=(t == 0), stop=(t == QT - 1))
                if grp % 2:
                    end_fill(ins, key)
                else:
                    ins.then_inc(av_half, 1)

            def heads_across(b):
                for i in range(2):
                    read_out(pe, ("av", b, i))
                for t in range(QT):
                    transposes(("avt", b, t), [(lambda d, g=g: d[:, g * P:(g + 1) * P], avT[:, g, t * P:(t + 1) * P])
                                               for g in range(NG)])

            def attention_across(b):
                for t in range(QT):
                    read_out(pe, ("avt", b, t))
                transposes(("aT", b), [(lambda d, k=k, t=t: d[:, k * S + t * P:k * S + (t + 1) * P], attn[:, t, k * P:(k + 1) * P])
                                       for k in range(KC) for t in range(QT)])

            def project(b):
                read_out(pe, ("aT", b))
                pe.wait_ge(ld_wout, 16)
                dst = begin_fill(pe, ("op", b))
                for t in range(QT):
                    for k in range(KC):
                        ins = pe.matmul(dst[:, t * C:(t + 1) * C], aT[:, k, t * P:(t + 1) * P], wout[:, k, :],
                                        start=(k == 0), stop=(k == KC - 1))
                end_fill(ins, ("op", b))

            def experts_in(b, f, name, w):
                dst = begin_fill(pe, (name, b, f))
                for i in range(2):
                    for k in range(KC):
                        ins = pe.matmul(dst[:, i * S:(i + 1) * S], w[:, k, 2 * f + i, :], x2T[:, b % 2, k, :],
                                        start=(k == 0), stop=(k == KC - 1))
                end_fill(ins, (name, b, f))

            def experts_out(b, t):
                dst = begin_fill(pe, ("y", b)) if t == 0 else bank[place[("y", b)][0]]
                if b == 0 and t == 0:
                    read_out(pe, ("wt", NWT - 1))
                    read_out(pe, ("wt", NWT - 2))
                for f in range(NF):
                    if t == 0 and f % 2 == 0:
                        pe.wait_ge(hid_done, NP2 * b + f // 2 + 1)
                    ins = pe.matmul(dst[:, t * C:(t + 1) * C], hid[:, f, t * P:(t + 1) * P], wdT[:, f, :],
                                    start=(f == 0), stop=(f == NF - 1))
                if t == QT - 1:
                    end_fill(ins, ("y", b))

            def tokens_across(b):
                pe.wait_ge(x2_done, QT * (b + 1))
                transposes(("x2t", b), [(lambda d, k=k, t=t: d[:, k * S + t * P:k * S + (t + 1) * P], x2[:, b % 2, t, k * P:(k + 1) * P])
                                        for k in range(KC) for t in range(QT)])

            def route(b):
                read_out(pe, ("x2t", b))
                dst = begin_fill(pe, ("rt", b))
                for t in range(QT):
                    for k in range(KC):
                        ins = pe.matmul(dst[:, t * 16:t * 16 + NW], x2T[:, b % 2, k, t * P:(t + 1) * P], gwT[:, k, :],
                                        start=(k == 0), stop=(k == KC - 1))
                end_fill(ins, ("rt", b))

            def route_across(b):
                pe.wait_ge(comb_done, 2 * (b + 1))
                transposes(("cT", b), [(lambda d, t=t: d[0:NW, t * P:(t + 1) * P], comb[:, t, :]) for t in range(QT)])

            query_scores(0, 0, NSF)
            maxima_across(0)
            for n in range(NWG):
                read_out(pe, ("wt", n))
            for b in range(B + 1):
                nxt, now, before = b + 1 < B, b < B, b > 0
                if now:
                    read_out(pe, ("mT", b))
                    for grp in range(NG + 1):
                        if grp < NG:
                            for j in range(4):
                                key_scores(b, 4 * grp + j)
                        if grp > 0:
                            attend(b, grp - 1)
                if b == 0:
                    pe.wait_ge(ld_gw, 32)
                    transposes(("gw",), [(lambda d, k=k: d[:, k * 16:k * 16 + NW], gw_nat[:, k * P:(k + 1) * P]) for k in range(KC)])
                if before:
                    experts_in(b - 1, 0, "g", wgT)
                if now:
                    heads_across(b)
                if before:
                    experts_in(b - 1, 0, "u", wuT)
                if now:
                    attention_across(b)
                if before:
                    experts_in(b - 1, 1, "g", wgT)
                if now:
                    project(b)
                    adjacency_transposes(b)
                if before:
                    experts_in(b - 1, 1, "u", wuT)
                if nxt:
                    query_scores(b + 1, 0, 2)
                if before:
                    experts_in(b - 1, 2, "g", wgT)
                    experts_in(b - 1, 2, "u", wuT)
                else:
                    for n in range(NWG, NWT):
                        weights_across(n)
                if nxt:
                    query_scores(b + 1, 2, 4)
                if before:
                    experts_in(b - 1, 3, "g", wgT)
                if nxt:
                    query_scores(b + 1, 4, 7)
                if before:
                    experts_in(b - 1, 3, "u", wuT)
                if now:
                    tokens_across(b)
                if nxt:
                    query_scores(b + 1, 7, 10)
                if before:
                    experts_in(b - 1, 4, "g", wgT)
                if now:
                    if b == 0:
                        read_out(pe, ("gw",))
                    route(b)
                if nxt:
                    query_scores(b + 1, 10, 13)
                if before:
                    experts_in(b - 1, 4, "u", wuT)
                if nxt:
                    query_scores(b + 1, 13, NSF)
                    maxima_across(b + 1)
                if before:
                    experts_out(b - 1, 0)
                if now:
                    route_across(b)
                if before:
                    experts_out(b - 1, 1)


_INS = ['x', 'ctx_512', 'L0_attn_W_qkv', 'L0_attn_W_out', 'L0_attn_b_out', 'L0_xattn_Wq', 'L0_xattn_Wk',
        'L0_xattn_gamma_raw', 'L0_ffn_gate_w', 'L0_ffn_w_gate', 'L0_ffn_w_up', 'L0_ffn_w_down',
        'L0_ffn_sh_gate', 'L0_ffn_sh_up', 'L0_ffn_sh_down', 'L0_ffn_se_gate_w']
_OUTS = [((4, 256, 256), 'float32')]


def kernel(**inputs):
    import numpy as _np
    import concourse.bacc as _bacc
    from concourse import mybir as _mybir
    from concourse.bass_utils import run_bass_kernel_spmd as _run

    nc = _bacc.Bacc("TRN2", target_bir_lowering=False, num_devices=1)
    arrays, args = {}, []
    for name in _INS:
        a = _np.ascontiguousarray(inputs[name])
        arrays[f"in_{name}_dram"] = a
        args.append(nc.dram_tensor(f"in_{name}_dram", a.shape, _mybir.dt.from_np(a.dtype), kind="ExternalInput").ap())
    for i, (shape, dtype) in enumerate(_OUTS):
        dt = _mybir.dt.from_np(_np.dtype(dtype))
        args.append(nc.dram_tensor(f"out_{i}_dram", shape, dt, kind="ExternalOutput").ap())
    decoder_layer(nc, *args)
    r = _run(nc, [arrays], core_ids=[0])
    return r.results[0]["out_0_dram"]
```

```python
from contextlib import ExitStack

import concourse.bass as bass
from concourse import mybir

F32 = mybir.dt.float32
F32R = mybir.dt.float32r
BF16 = mybir.dt.bfloat16
I32 = mybir.dt.int32
U32 = mybir.dt.uint32
ALU = mybir.AluOpType
ACT = mybir.ActivationFunctionType
AX = mybir.AxisListType

P = 128
FP8_MAX = 448.0
LN_EPS = 1e-5
TOP_K_RATIO = 0.3
E4M3_LEAST_NORMAL = 2.0 ** -6
E4M3_ROUNDER = 1.5 * 2.0 ** 20
EXPONENT_BITS = 0x7F800000
LOWEST = -3.0e38
WARM = 9


def decoder_layer(nc, x, ctx_512, W_qkv, W_out, b_out, Wq, Wk, gamma_raw, gate_w, w_gate, w_up, w_down,
                  sh_gate, sh_up, sh_down, se_gate_w, out):
    B, S, C = x.shape
    TOK = B * S
    NT = TOK // P
    QT = S // P
    KC = C // P
    NH = 16
    HD = C // NH
    HG = P // HD
    D = ctx_512.shape[2]
    SIM_HEADS = 4
    SIM_SCALE = 1.0 / ((D // SIM_HEADS) ** 0.5 * SIM_HEADS)
    TOPK = max(1, int(S * TOP_K_RATIO))
    ROUNDS = (TOPK + 7) // 8
    NE, HM, _ = w_gate.shape
    HS = sh_gate.shape[0]
    NS = HS // P
    NF = NE + NS
    NW = NE + 1
    SLOT = 32
    NG = NH // 4
    ER = 8
    NSF = KC * QT * HG // 2
    assert HM == P and QT == 2 and KC == 2 and D == 64

    es = ExitStack()
    with es:
        def sb(name, shape, dt=F32):
            return es.enter_context(nc.sbuf_tensor(name, shape, dt))

        def sem(name):
            return es.enter_context(nc.semaphore(name))

        x_sb = sb("x_sb", [P, NT, C])
        with nc.sbuf_tensor("ctx_sb", [P, NT, D], F32) as ctx_sb:
            pass
        x2low = sb("x2low", [P, KC, S], F32R)
        wc_sb = sb("wc_sb", [D, 2, D])
        place_qkv = sb("wqkv_avT_attn", [P, 3 * KC * C])
        wqkv = place_qkv[:].rearrange("p (k f) -> p k f", k=KC)
        wout = sb("wout", [P, KC, C])
        bout = sb("bout", [P, C])
        place_gu = sb("wgu_expo_silu", [P, 2 * NF * C])
        wg_nat = place_gu[:, 0:NF * C].rearrange("p (f c) -> p f c", f=NF)
        wu_nat = place_gu[:, NF * C:2 * NF * C].rearrange("p (f c) -> p f c", f=NF)
        place_d = sb("wd_hid", [P, NF * C])
        wd_nat = place_d[:].rearrange("p (k f h) -> p k f h", k=KC, f=NF)
        gw_nat = sb("gw_nat", [NW, C])
        graw = sb("graw", [P, 1])

        ident = sb("ident", [P, P])
        identb = sb("identb", [P, P], BF16)
        ones = sb("ones", [P, P])
        headmask = sb("headmask", [P, HG])
        sel = sb("sel", [P, NH, P], BF16)
        iota = sb("iota", [P, NE])
        wcT = sb("wcT", [P, 2, P])
        with nc.sbuf_tensor("xT_ctxT_qkcT_wgT_wuT", [P, 5 * TOK], F32) as place_t:
            pass
        wlow = sb("wlow", [P, 2 * KC * NF * P], F32R)
        with nc.sbuf_tensor("qkraw_vraw", [P, 4 * TOK + NT * C], F32) as place_raw:
            pass
        whigh = sb("whigh", [P, 2 * KC * NF * P], F32R)
        sb("vraw_rest", [P, 4 * TOK + NT * C - 2 * KC * NF * P])
        qkraw = place_raw[:, 0:4 * TOK].rearrange("p (q k s) -> p q k s", q=2, k=KC)
        vraw = place_raw[:, 4 * TOK:4 * TOK + NT * C].rearrange("p (t c) -> p t c", t=NT)
        xT = place_t[:, 0:KC * TOK].rearrange("p (k s) -> p k s", k=KC)
        ctxT = place_t[:, KC * TOK:(KC + 1) * TOK]
        qkcT = place_t[:, (KC + 1) * TOK:(KC + 3) * TOK].rearrange("p (k s) -> p k s", k=2)
        sim = sb("sim", [P, NT, S])
        work = sb("work", [P, QT, S])
        top8 = sb("top8", [P, QT, 8])
        sig = sb("sig", [P, QT, S])
        adj = sb("adj", [P, QT, S])
        adjs = sb("adjs", [P, QT, S])
        gam = sb("gam", [P, 5])

        amax = sb("amax", [P, 3, 4])
        amax3 = sb("amax3", [P, 3])
        gmax = sb("gmax", [2, 1])
        gmaxv = sb("gmaxv", [1, 1])
        gdiag = sb("gdiag", [2, 2])
        scale3 = sb("scale3", [P, 3])
        inv3 = sb("inv3", [P, 3])
        cexp = sb("cexp", [P, 1])

        qs = sb("qs", [P, 3, 2 * S])
        qm = sb("qm", [P, 3, 2 * S])
        k8 = sb("k8", [P, KC, S], BF16)
        q8 = sb("q8", [P, 2, KC, S], BF16)
        kmask = sb("kmask", [P, 2, NH, S], BF16)
        v8 = sb("v8", [P, 2, QT, NH, SLOT])
        negm = sb("negm", [P, QT, NH])
        mparts = sb("mparts", [P, QT, P], BF16)
        mT = sb("mT", [P, 2, S], BF16)
        warm = mT[:].rearrange("p b s -> p (b s)")
        expo = place_gu[:, 0:ER * QT * S].rearrange("p (h t s) -> p h t s", h=ER, t=QT)
        avT = place_qkv[:, 0:NG * S].rearrange("p (g s) -> p g s", g=NG)
        rsum = sb("rsum", [P, QT, NH])
        attn = place_qkv[:, NG * S:NG * S + QT * C].rearrange("p (t c) -> p t c", t=QT)
        aT = sb("aT", [P, KC, S])
        pre1 = sb("pre1", [P, QT, C])
        pre2 = sb("pre2", [P, QT, C])
        x2 = sb("x2", [P, 2, QT, C])
        yo = sb("yo", [P, 2, QT, C])
        stats = sb("stats", [P, 3, QT, 6])
        mv = sb("mv", [P, 3, QT, 2])
        vare = sb("vare", [P, 3, QT])
        halfneg = sb("halfneg", [P, QT])
        rstd = sb("rstd", [P, 3, QT])
        rg = sb("rg", [P, QT])

        wgT = place_t[:, 0:KC * NF * P].rearrange("p (k f h) -> p k f h", k=KC, f=NF)
        wuT = place_t[:, KC * NF * P:2 * KC * NF * P].rearrange("p (k f h) -> p k f h", k=KC, f=NF)
        SPLIT = 2
        wghigh, wuhigh, wglow, wulow = (m[:, i * KC * NF * P:(i + 1) * KC * NF * P].rearrange("p (k f h) -> p k f h", k=KC, f=NF)
                                        for m in (whigh, wlow) for i in range(2))
        x2high = sb("x2high", [P, KC, S], F32R)
        wdT = sb("wdT", [P, NF, C])
        gwT = sb("gwT", [P, KC, NW])
        x2T = sb("x2T", [P, 2, KC, S])
        rsc = sb("rsc", [P, QT, NW])
        rtop = sb("rtop", [P, QT, 8])
        ridx = sb("ridx", [P, QT, 8], U32)
        ridf = sb("ridf", [P, QT, 2])
        rarg = sb("rarg", [P, QT, 2])
        rtanh = sb("rtanh", [P, QT, 2])
        rw = sb("rw", [P, QT, 2])
        rw2 = sb("rw2", [P, QT, 1])
        hot = sb("hot", [P, QT, 2, NE])
        comb = sb("comb", [P, QT, NW])
        combT = sb("combT", [NW, S])
        cb = sb("cb", [P, NW, S])
        silu = place_gu[:, ER * QT * S:ER * QT * S + 4 * S].rearrange("p (n f s) -> p n f s", n=2, f=2)
        RING = 4
        hid1 = sb("hid1", [P, RING, 2, S])
        hid = place_d[:].rearrange("p (f s) -> p f s", f=NF)
        comb_dram = nc.dram_tensor("comb_dram", (B, NW, S), F32, kind="Internal").ap()

        bank = {n: es.enter_context(nc.psum_tensor(n, [P, 512], F32))
                for n in ("SA0", "SA1", "ST0", "ST1", "AV0", "AV1", "MG", "MU")}

        filled = {n: sem("filled_" + n) for n in bank}
        emptied = {n: sem("emptied_" + n) for n in bank}
        place, count = {}, {n: 0 for n in bank}

        def plan(key, name):
            place[key] = (name, count[name])
            count[name] += 1

        four = ("AV0", "AV1", "MG", "MU")
        NWT = 3 * KC * NF // 4
        NWG = 2 * KC * NF // 4
        plan(("cw",), "SA0")
        plan(("ct", 0), "SA1")
        plan(("cq", 0, 0), "SA0")
        plan(("cq", 1, 0), "ST0")
        plan(("sim", 0), "SA1")
        plan(("sim", 1), "SA0")
        plan(("ct", 1), "SA1")
        plan(("cq", 0, 1), "SA0")
        plan(("cq", 1, 1), "ST0")
        plan(("sim", 2), "ST0")
        early = [("xt", 0), ("xt", 1), ("qk", 0), ("qk", 1), ("xt", 2), ("xt", 3)]
        early += [("qk", n) for n in range(2, 8)] + [("v", n) for n in range(4)] + [("wt", n) for n in range(NWG)]
        for n, key in enumerate(early):
            plan(key, four[n % 4])
        for n in range(4):
            plan(("mx", n), "ST1")
        plan(("sim", 3), "ST1")
        for b in range(B):
            for h in range(NH):
                plan(("st", b, h), ("ST0", "ST1")[h % 2])
            plan(("av", b, 0), "AV0")
            plan(("av", b, 1), "AV0")
        for b in range(2):
            for i in range(NSF):
                plan(("s", b, i), ("SA0", "SA1")[i % 2])
            plan(("mT", b), "SA0")
        for b in range(B):
            if 1 < b + 1 < B:
                plan(("mT", b + 1), "SA0")
            plan(("at", b), "SA0")
            plan(("avt", b, 1), "SA1")
            if b + 2 < B:
                for i in range(NSF):
                    plan(("s", b + 2, i), ("SA0", "SA1")[i % 2])
        for b in range(B):
            for name in ("avt", "aT", "op", "x2t", "rt", "cT"):
                plan((name, b, 0) if name == "avt" else (name, b), "AV1")
        plan(("gw",), "MG")
        for n in range(NWG, NWT):
            plan(("wt", n), ("MU", "MG")[n % 2])
        for b in range(B):
            for f in range(NF // 2):
                plan(("g", b, f), "MG")
                plan(("u", b, f), "MU")
            for t in range(QT):
                plan(("y", b, t), (("MG", "MU") if b + 1 < B else ("SA0", "SA1"))[t])
        emitted = {n: 0 for n in bank}

        def begin_fill(pe, key):
            name, n = place[key]
            assert emitted[name] == n, (key, name)
            emitted[name] += 1
            if n:
                pe.wait_ge(emptied[name], n)
            return bank[name]

        def end_fill(ins, key):
            ins.then_inc(filled[place[key][0]], 1)

        def full(eng, key):
            name, n = place[key]
            eng.wait_ge(filled[name], n + 1)
            return bank[name]

        def release(ins, key):
            ins.then_inc(emptied[place[key][0]], 1)

        def read_out(eng, key):
            name, n = place[key]
            eng.wait_ge(emptied[name], n + 1)

        ld_ctx, ld_wc, ld_small = [sem(f"ld_ctx{i}") for i in range(2)], sem("ld_wc"), sem("ld_small")
        ld_wqk, ld_wv = sem("ld_wqk"), sem("ld_wv")
        ld_x = [sem(f"ld_x{i}") for i in range(2)]
        ld_wg, ld_wu, ld_wd, ld_gw, ld_wout = sem("ld_wg"), sem("ld_wu"), sem("ld_wd"), sem("ld_gw"), sem("ld_wout")
        const_step, consts = sem("const_step"), sem("consts")
        bias_added = sem("bias_added")
        gate_exp = sem("gamma_exp")
        tanh_done, topk_step, adj_done = sem("tanh_done"), sem("topk_step"), sem("adj_done")
        amax_done, gmax_done = sem("amax_done"), sem("gmax_done")
        scales_done = sem("scales_done")
        scaled = [sem(f"scaled_{n}") for n in "qkv"]
        rounders_done = [sem(f"rounders_{n}_done") for n in "qkv"]
        quantized = [sem(f"quantized_{n}") for n in "qkv"]
        km_done = [sem(f"kmask{g}_done") for g in range(KC)]
        sums_done = sem("rounder_sums_done")
        warm_set = sem("warm_set")
        mparts_done = sem("mparts_done")
        av_half = sem("av_half")
        attn_done = sem("attn_done")
        ve_s = [sem(f"var_eps{i}_done") for i in range(3)]
        rstd_s = [sem(f"rstd{i}_done") for i in range(3)]
        x2_done = sem("x2_done")
        whigh_done, wlow_done, xhigh_done = sem("weights_high_done"), sem("weights_low_done"), sem("x2_high_done")
        rarg_done, rtanh_done, comb_done = sem("router_arg_done"), sem("router_tanh_done"), sem("comb_done")
        comb_written, cb_done = sem("comb_written"), sem("cb_done")
        silu_done, hid_done = sem("silu_done"), sem("hid_done")
        yo_done, out_done = sem("yo_done"), [sem(f"out_done{i}") for i in range(2)]
        dve_step = sem("dve_step")

        NP2 = NF // 2
        cuts_s = (0, 2, 4, 6, 7, 9, 11, 13, 14, 16, 16)
        assert len(cuts_s) == 2 * NP2 + 1 and cuts_s[-1] == NSF
        block = es.enter_context(nc.Block())

        @block.sync
        def _(sp):
            cv = ctx_512.rearrange("b (t p) d -> p (b t) d", p=P)
            xv = x.rearrange("b (t p) c -> p (b t) c", p=P)
            wv = W_qkv.rearrange("(k p) f -> p k f", p=P)
            sp.dma_start(ctx_sb[:, 0:NT // 2, :], cv[:, 0:NT // 2, :]).then_inc(ld_ctx[0], 16)
            sp.dma_start(wc_sb[:, 0, :], Wq).then_inc(ld_wc, 16)
            sp.dma_start(wc_sb[:, 1, :], Wk).then_inc(ld_wc, 16)
            sp.dma_start(x_sb[:, 0:NT // 2, :], xv[:, 0:NT // 2, :]).then_inc(ld_x[0], 16)
            sp.dma_start(wqkv[:, :, 0:2 * C], wv[:, :, 0:2 * C]).then_inc(ld_wqk, 16)
            sp.dma_start(x_sb[:, NT // 2:NT, :], xv[:, NT // 2:NT, :]).then_inc(ld_x[1], 16)
            sp.dma_start(graw[:], gamma_raw.rearrange("(a c) -> a c", a=1).broadcast_to((P, 1))).then_inc(ld_small, 16)
            sp.dma_start(wqkv[:, :, 2 * C:3 * C], wv[:, :, 2 * C:3 * C]).then_inc(ld_wv, 16)
            sp.dma_start(ctx_sb[:, NT // 2:NT, :], cv[:, NT // 2:NT, :]).then_inc(ld_ctx[1], 16)
            sp.dma_start(bout[:], b_out.rearrange("(a c) -> a c", a=1).broadcast_to((P, C))).then_inc(ld_small, 16)
            sp.dma_start(wg_nat[:, 0:NE, :], w_gate.rearrange("e h c -> h e c")).then_inc(ld_wg, 16)
            sp.dma_start(wg_nat[:, NE:NF, :], sh_gate.rearrange("(s h) c -> h s c", h=P)).then_inc(ld_wg, 16)
            sp.dma_start(wu_nat[:, 0:NE, :], w_up.rearrange("e h c -> h e c")).then_inc(ld_wu, 16)
            sp.dma_start(wu_nat[:, NE:NF, :], sh_up.rearrange("(s h) c -> h s c", h=P)).then_inc(ld_wu, 16)
            for k in range(KC):
                sp.dma_start(wd_nat[:, k, 0:NE, :], w_down[:, k * P:(k + 1) * P, :].rearrange("e c h -> c e h")).then_inc(ld_wd, 16)
                sp.dma_start(wd_nat[:, k, NE:NF, :], sh_down[k * P:(k + 1) * P, :].rearrange("c (s h) -> c s h", h=P)).then_inc(ld_wd, 16)
            sp.dma_start(gw_nat[0:NE, :], gate_w).then_inc(ld_gw, 16)
            sp.dma_start(gw_nat[NE:NW, :], se_gate_w).then_inc(ld_gw, 16)
            sp.dma_start(wout[:], W_out.rearrange("(k p) o -> p k o", p=P)).then_inc(ld_wout, 16)
            for b in range(B + 1):
                if b < B:
                    read_out(sp, ("cT", b))
                    sp.dma_start(comb_dram[b], combT[:]).then_inc(comb_written, 16)
                    sp.wait_ge(comb_written, 16 * (b + 1))
                    if b >= 1:
                        sp.wait_ge(hid_done, NP2 * b)
                    sp.dma_start(cb[:, :, :], comb_dram[b:b + 1].broadcast_to((P, NW, S))).then_inc(cb_done, 16)
                if b >= 1:
                    for t in range(QT):
                        sp.wait_ge(yo_done, QT * (b - 1) + t + 1)
                        sp.dma_start(out[b - 1, t * P:(t + 1) * P, :], yo[:, (b - 1) % 2, t, :]).then_inc(out_done[(b - 1) % 2], 16)
            for i in range(2):
                sp.wait_ge(out_done[i], 16 * QT * (B // 2))
            sp.wait_ge(cb_done, 16 * B)

        @block.gpsimd
        def _(pool):
            pool.memset(ident[:], 0.0).then_inc(const_step, 1)
            pool.memset(wcT[:], 0.0).then_inc(consts, 1)
            pool.memset(ctxT, 0.0).then_inc(consts, 1)
            pool.wait_ge(const_step, 1)
            pool.affine_select(out=ident[:], in_=ident[:], compare_op=ALU.not_equal, fill=1.0, base=0,
                               pattern=[[-1, P]], channel_multiplier=1).then_inc(consts, 1)
            pool.memset(identb[:], 0.0).then_inc(const_step, 1)
            pool.memset(headmask[:], 1.0).then_inc(const_step, 1)
            pool.memset(sel[:], 0.0).then_inc(const_step, 1)
            pool.wait_ge(const_step, 4)
            pool.affine_select(out=identb[:], in_=identb[:], compare_op=ALU.not_equal, fill=1.0, base=0,
                               pattern=[[-1, P]], channel_multiplier=1).then_inc(consts, 1)
            pool.affine_select(out=headmask[:], in_=headmask[:], compare_op=ALU.is_ge, fill=0.0, base=0,
                               pattern=[[-HD, HG]], channel_multiplier=1).then_inc(const_step, 1)
            pool.affine_select(out=sel[:], in_=sel[:], compare_op=ALU.not_equal, fill=1.0, base=0,
                               pattern=[[-1, NH], [0, P]], channel_multiplier=1).then_inc(const_step, 1)
            pool.wait_ge(const_step, 6)
            pool.affine_select(out=headmask[:], in_=headmask[:], compare_op=ALU.is_ge, fill=0.0, base=HD - 1,
                               pattern=[[HD, HG]], channel_multiplier=-1).then_inc(consts, 1)
            pool.affine_select(out=sel[:], in_=sel[:], compare_op=ALU.not_equal, fill=1.0, base=-NH,
                               pattern=[[-1, NH], [0, P]], channel_multiplier=1).then_inc(consts, 1)
            pool.memset(ones[:], 1.0).then_inc(consts, 1)
            pool.memset(v8[:], 1.0).then_inc(consts, 1)
            pool.memset(mparts[:], 0.0).then_inc(consts, 1)
            pool.memset(halfneg[:], -0.5).then_inc(const_step, 1)
            pool.wait_ge(consts, 9)
            pool.wait_ge(const_step, 7)

            sums = [0]

            def on_grid(b, kind):
                pool.wait_ge(rounders_done[kind], b + 1)
                pool.tensor_tensor(qs[:, kind, :], qs[:, kind, :], qm[:, kind, :], ALU.add).then_inc(sums_done, 1)
                sums[0] += 1
                pool.wait_ge(sums_done, sums[0])
                if kind == 2:
                    if b >= 2:
                        full(pool, ("av", b - 2, 1))
                    dst, form = v8[:, b % 2, :, :, 0:HD], dict(t=QT, h=NH)
                    a, c = (m[:, 2, :].rearrange("p (t h d) -> p t h d", **form) for m in (qs, qm))
                else:
                    if kind == 0 and b >= 2:
                        full(pool, ("st", b - 2, NH - 1))
                    if kind == 1:
                        for g in range(KC):
                            pool.wait_ge(km_done[g], HG * b)
                    dst = q8[:, b % 2] if kind == 0 else k8[:, :, :]
                    a, c = (m[:, kind, :].rearrange("p (k s) -> p k s", k=KC) for m in (qs, qm))
                pool.tensor_tensor(dst, a, c, ALU.subtract).then_inc(quantized[kind], 1)

            def inv_std(i, n, first=0, last=QT):
                pool.wait_ge(ve_s[i], n)
                pool.tensor_tensor(rstd[:, i, first:last], vare[:, i, first:last], halfneg[:, first:last], ALU.pow).then_inc(rstd_s[i], 1)

            def weigh_hidden(b, f):
                if f == 0:
                    pool.wait_ge(cb_done, 16 * (b + 1))
                    if b >= 1:
                        full(pool, ("y", b - 1, QT - 1))
                    else:
                        full(pool, ("wt", NWT - 1))
                        full(pool, ("wt", NWT - 2))
                n = b * NP2 + f
                read_out(pool, ("u", b, f))
                for i in range(2):
                    e = min(2 * f + i, NE)
                    ins = pool.tensor_tensor(hid[:, 2 * f + i, :], hid1[:, n % RING, i, :], cb[:, e, :], ALU.mult)
                ins.then_inc(hid_done, 1)

            on_grid(0, 0)
            on_grid(1, 1)
            on_grid(1, 0)
            on_grid(0, 2)
            on_grid(1, 2)
            pool.wait_ge(ld_small, 32)
            for n in range(4):
                full(pool, ("xt", n))
            for t in range(NT):
                pool.tensor_tensor(x_sb[:, t, :], x_sb[:, t, :], bout[:], ALU.add).then_inc(bias_added, 1)
            for b in range(B):
                if b + 2 < B:
                    on_grid(b + 2, 1)
                if b == SPLIT:
                    full(pool, ("g", b - 1, NP2 - 1))
                    full(pool, ("u", b - 1, NP2 - 1))
                    for n in range(NWG):
                        pool.wait_ge(whigh_done, n + 1)
                        part = slice(n * 512, (n + 1) * 512)
                        pool.tensor_tensor(wlow[:, part], place_t[:, part], whigh[:, part].bitcast(F32),
                                           ALU.subtract).then_inc(wlow_done, 1)
                inv_std(0, b + 1)
                if b + 2 < B:
                    on_grid(b + 2, 0)
                inv_std(1, b + 1)
                if b + 2 < B:
                    on_grid(b + 2, 2)
                if b > 0:
                    inv_std(2, QT * (b - 1) + 1, 0, 1)
                    inv_std(2, QT * b, 1, QT)
                for f in range(NP2):
                    weigh_hidden(b, f)
            for t in range(QT):
                inv_std(2, QT * (B - 1) + t + 1, t, t + 1)

        @block.scalar
        def _(act):
            def context_across(hf):
                src = full(act, ("ct", hf))
                release(act.copy(ctxT[0:D, hf * 512:(hf + 1) * 512], src[0:D, :]), ("ct", hf))

            def context_qk(hf):
                for kind in range(2):
                    src = full(act, ("cq", kind, hf))
                    release(act.copy(qkcT[:, kind, hf * 512:(hf + 1) * 512], src[:, :]), ("cq", kind, hf))

            def similarities(b):
                src = full(act, ("sim", b))
                release(act.mul(sim[:, QT * b:QT * (b + 1), :], src[:, :].rearrange("p (t s) -> p t s", t=QT), SIM_SCALE), ("sim", b))

            def x_across(n):
                src = full(act, ("xt", n))
                release(act.copy(xT[:, n % 2, (n // 2) * 512:(n // 2 + 1) * 512], src[:, :]), ("xt", n))

            def qk_out(n):
                hf, kind, g = n // 4, (n // 2) % 2, n % 2
                src = full(act, ("qk", n))
                release(act.copy(qkraw[:, kind, g, hf * 512:(hf + 1) * 512], src[:, :]), ("qk", n))

            def tanh_sim(b):
                read_out(act, ("sim", b))
                if b >= 1:
                    act.wait_ge(adj_done, QT * b)
                act.activation(sig[:, :, :], sim[:, QT * b:QT * (b + 1), :], ACT.Tanh, scale=0.5).then_inc(tanh_done, 1)

            def scale_qkv(b, kind):
                act.wait_ge(scales_done, 2 if kind < 2 else 3)
                if b >= 1:
                    act.wait_ge(quantized[kind], b)
                src = qkraw[:, kind, :, b * S:(b + 1) * S] if kind < 2 else vraw[:, QT * b:QT * (b + 1), :]
                act.activation(qs[:, kind, :].rearrange("p (t s) -> p t s", t=2), src, ACT.Copy,
                               scale=inv3[:, kind:kind + 1]).then_inc(scaled[kind], 1)

            def weights_out(n):
                src = full(act, ("wt", n))
                dst = (place_t[:, 0:KC * NF * P], place_t[:, KC * NF * P:2 * KC * NF * P],
                       wdT[:].rearrange("p f c -> p (f c)"))[n // (NWT // 3)]
                m = n % (NWT // 3)
                release(act.copy(dst[:, m * 512:(m + 1) * 512], src[:, :]), ("wt", n))

            def values_out(n):
                src = full(act, ("v", n))
                release(act.copy(vraw[:, 2 * n:2 * n + 2, :], src[:, :].rearrange("p (t c) -> p t c", t=2)), ("v", n))

            def spread_keys(b, g, first=0, last=HG):
                if first == 0:
                    act.wait_ge(consts, 9)
                    act.wait_ge(quantized[1], b + 1)
                    if b >= 2:
                        full(act, ("st", b - 2, NH - 1))
                for h in range(first, last):
                    act.activation(kmask[:, b % 2, g * HG + h, :], k8[:, g, :], ACT.Copy,
                                   scale=headmask[:, h:h + 1]).then_inc(km_done[g], 1)

            def exponentials(b, first, last):
                for h in range(first, last):
                    src = full(act, ("st", b, h))
                    grp = (b * NH + h) // 4 - ER // 4
                    if grp >= 0 and grp % 2 == 0:
                        act.wait_ge(av_half, grp // 2 + 1)
                    elif grp >= 0:
                        full(act, ("av", grp // NG, grp % NG // 2))
                    release(act.activation(expo[:, h % ER, :, :], src[:, :].rearrange("p (t s) -> p t s", t=QT), ACT.Exp,
                                           scale=cexp[:, 0:1]), ("st", b, h))

            def attended(b, i):
                src = full(act, ("av", b, i))
                if b >= 1 and i == 0:
                    full(act, ("avt", b - 1, QT - 1))
                release(act.copy(avT[:, 2 * i:2 * i + 2, :], src[:, :].rearrange("p (g s) -> p g s", g=2)), ("av", b, i))

            def attention_across(b):
                src = full(act, ("aT", b))
                if b >= 1:
                    full(act, ("op", b - 1))
                release(act.copy(aT[:, :, :], src[:, :].rearrange("p (k s) -> p k s", k=KC)), ("aT", b))

            def high_weights(n):
                if n == 0:
                    for kind in range(3):
                        act.wait_ge(scaled[kind], B)
                act.activation(whigh[:, n * 512:(n + 1) * 512], place_t[:, n * 512:(n + 1) * 512],
                               ACT.Copy).then_inc(whigh_done, 1)

            def silus(b, f):
                n = b * NP2 + f
                src = full(act, ("g", b, f))
                if n >= 2:
                    read_out(act, ("u", (n - 2) // NP2, (n - 2) % NP2))
                release(act.activation(silu[:, n % 2, :, :], src[:, :].rearrange("p (f s) -> p f s", f=2),
                                       ACT.Silu), ("g", b, f))

            act.wait_ge(warm_set, 1)
            act.activation(gam[:, 1:2], warm[:, 0:1], ACT.Exp)
            act.wait_ge(consts, 2)
            src = full(act, ("cw",))
            release(act.copy(wcT[0:D, :, 0:D], src[0:D, 0:2 * D].rearrange("p (k d) -> p k d", k=2)), ("cw",))
            context_across(0)
            context_qk(0)
            x_across(0)
            similarities(0)
            qk_out(0)
            similarities(1)
            qk_out(1)
            x_across(2)
            act.wait_ge(ld_small, 32)
            act.activation(gam[:, 0:1], graw[:, :], ACT.Exp, scale=-1.0).then_inc(gate_exp, 1)
            for n in range(2, 8):
                qk_out(n)
                if n == 4:
                    tanh_sim(0)
            values_out(0)
            context_across(1)
            scale_qkv(0, 1)
            scale_qkv(0, 0)
            for n in range(1, 4):
                values_out(n)
            context_qk(1)
            act.wait_ge(km_done[0], 4)
            spread_keys(0, 0, 4, HG)
            similarities(2)
            spread_keys(0, 1, 0, 4)
            scale_qkv(1, 1)
            spread_keys(0, 1, 4, HG)
            similarities(3)
            weights_out(0)
            weights_out(1)
            scale_qkv(0, 2)
            scale_qkv(1, 0)
            weights_out(2)
            weights_out(3)
            spread_keys(1, 0, 0, 4)
            weights_out(4)
            weights_out(5)
            spread_keys(1, 0, 4, HG)
            for n in range(6, NWG):
                weights_out(n)
            exponentials(0, 0, 8)
            scale_qkv(1, 2)
            exponentials(0, 8, 12)
            attended(0, 0)
            exponentials(0, 12, NH)
            attended(0, 1)

            for b in range(B):
                nxt, second = b + 1 < B, b + 2 < B
                if second:
                    scale_qkv(b + 2, 1)
                if nxt:
                    exponentials(b + 1, 0, 4)
                if nxt:
                    attention_across(b)
                if nxt:
                    exponentials(b + 1, 4, 6)
                if b == 0:
                    src = full(act, ("gw",))
                    release(act.copy(gwT[:, :, :], src[:, 0:KC * 16].rearrange("p (k n) -> p k n", k=KC)[:, :, 0:NW]), ("gw",))
                    weights_out(NWG)
                if nxt:
                    exponentials(b + 1, 6, 8)
                if second:
                    scale_qkv(b + 2, 0)
                if nxt:
                    tanh_sim(b + 1)
                if second:
                    scale_qkv(b + 2, 2)
                if b == 0:
                    weights_out(NWG + 1)
                if nxt:
                    exponentials(b + 1, 8, 12)
                    attended(b + 1, 0)
                if b == 0:
                    weights_out(NWG + 2)
                if nxt:
                    exponentials(b + 1, 12, NH)
                if b == 0:
                    weights_out(NWG + 3)
                    weights_out(NWG + 4)
                src = full(act, ("x2t", b))
                src = src[:, :].rearrange("p (k s) -> p k s", k=KC)
                if b < SPLIT:
                    release(act.copy(x2T[:, b % 2, :, :], src), ("x2t", b))
                else:
                    act.copy(x2high[:, :, :], src).then_inc(xhigh_done, 1)
                if second and b > 0:
                    spread_keys(b + 2, 0, 0, 4)
                act.wait_ge(rarg_done, 2 * (b + 1))
                act.activation(rtanh[:, :, :], rarg[:, :, :], ACT.Tanh, scale=0.5).then_inc(rtanh_done, 1)
                if second and b > 0:
                    spread_keys(b + 2, 0, 4, HG)
                if nxt:
                    attended(b + 1, 1)
                silus(b, 0)
                src = full(act, ("cT", b))
                if b >= 1:
                    act.wait_ge(comb_written, 16 * b)
                release(act.copy(combT[:, :], src[0:NW, 0:S]), ("cT", b))
                if second:
                    spread_keys(b + 2, 1)
                for f in range(1, NP2):
                    if b + 1 == SPLIT:
                        for n in range(NWG * (f - 1) // (NP2 - 1), NWG * f // (NP2 - 1)):
                            high_weights(n)
                    silus(b, f)
                    if b + 2 == B and f == 3:
                        attention_across(b + 1)

        @block.vector
        def _(dve):
            steps = [0]

            def step(ins):
                ins.then_inc(dve_step, 1)
                steps[0] += 1
                return steps[0]

            def after(n):
                dve.wait_ge(dve_step, n)

            dve.memset(warm, 0.0).then_inc(warm_set, 1)
            for e in range(NE):
                dve.memset(iota[:, e:e + 1], float(e))

            def topk_rounds(b, first, last):
                base = b * (4 * ROUNDS - 2)
                if first == 0:
                    read_out(dve, ("sim", b))
                    if b >= 1:
                        dve.wait_ge(adj_done, QT * b)
                for r in range(first, last):
                    for t in range(QT):
                        if r > 0:
                            dve.wait_ge(topk_step, base + 4 * (r - 1) + 3 + t)
                        src = work[:, t, :] if r else sim[:, QT * b + t, :]
                        dve.max(top8[:, t, :], src).then_inc(topk_step, 1)
                    if r + 1 < ROUNDS:
                        for t in range(QT):
                            dve.wait_ge(topk_step, base + 4 * r + 1 + t)
                            src = work[:, t, :] if r else sim[:, QT * b + t, :]
                            dve.match_replace(work[:, t, :], top8[:, t, :], src, LOWEST).then_inc(topk_step, 1)

            def adjacency(b):
                dve.wait_ge(tanh_done, b + 1)
                after(gamma_step)
                n = step(dve.tensor_scalar(sig[:, :, :], sig[:, :, :], gam[:, 3:4], gam[:, 3:4], ALU.mult, ALU.add))
                dve.wait_ge(topk_step, (b + 1) * (4 * ROUNDS - 2))
                after(n)
                least = (TOPK - 1) % 8
                for t in range(QT):
                    dve.scalar_tensor_tensor(out=adj[:, t, :], in0=sim[:, QT * b + t, :], scalar=top8[:, t, least:least + 1],
                                             in1=sig[:, t, :], op0=ALU.is_ge, op1=ALU.mult).then_inc(adj_done, 1)

            def adjacency_sum(b):
                src = full(dve, ("at", b))
                release(dve.tensor_tensor(adjs[:, :, :], src[:, :].rearrange("p (t s) -> p t s", t=QT),
                                          adj[:, :, :], ALU.add), ("at", b))

            def gamma_factors():
                dve.wait_ge(gate_exp, 1)
                n = step(dve.tensor_scalar(gam[:, 1:2], gam[:, 0:1], 1.0, None, ALU.add))
                after(n)
                n = step(dve.reciprocal(gam[:, 2:3], gam[:, 1:2]))
                after(n)
                step(dve.tensor_scalar(gam[:, 3:4], gam[:, 2:3], 0.25, None, ALU.mult))
                return step(dve.tensor_scalar(gam[:, 4:5], gam[:, 2:3], -1.0, 2.0, ALU.mult, ALU.add))

            def x_across(n):
                src = full(dve, ("xt", n))
                release(dve.tensor_copy(xT[:, n % 2, (n // 2) * 512:(n // 2 + 1) * 512], src[:, :]), ("xt", n))

            def abs_max(kind, j, key, src):
                read_out(dve, key)
                return step(dve.tensor_reduce(amax[:, kind, j:j + 1], src, AX.X, ALU.max, apply_absolute_value=True))

            def rounders(b, kind):
                dve.wait_ge(scaled[kind], b + 1)
                n = step(dve.tensor_scalar(qm[:, kind, :].bitcast(I32), qs[:, kind, :].bitcast(I32), EXPONENT_BITS, None,
                                           ALU.bitwise_and))
                after(n)
                dve.tensor_scalar(qm[:, kind, :], qm[:, kind, :], E4M3_LEAST_NORMAL, E4M3_ROUNDER,
                                  ALU.max, ALU.mult).then_inc(rounders_done[kind], 1)

            def quantize_first():
                rounders(0, 1)
                rounders(0, 0)
                dve.wait_ge(rounders_done[1], 1)
                n = step(dve.tensor_tensor(qs[:, 1, :], qs[:, 1, :], qm[:, 1, :], ALU.add))
                after(n)
                dve.tensor_tensor(k8[:, :, :], qs[:, 1, :].rearrange("p (k s) -> p k s", k=KC),
                                  qm[:, 1, :].rearrange("p (k s) -> p k s", k=KC), ALU.subtract).then_inc(quantized[1], 1)

            def spread_keys(b, g, first, last):
                dve.wait_ge(consts, 9)
                dve.wait_ge(quantized[1], b + 1)
                if b >= 2:
                    full(dve, ("st", b - 2, NH - 1))
                for h in range(first, last):
                    dve.tensor_scalar(kmask[:, b % 2, g * HG + h, :], k8[:, g, :], headmask[:, h:h + 1], None,
                                      ALU.mult).then_inc(km_done[g], 1)

            def row_maxima(b, first, last):
                for i in range(first, last):
                    g, t, hp = i // (2 * HG // 2), (i // (HG // 2)) % 2, i % (HG // 2)
                    h = g * HG + 2 * hp
                    src = full(dve, ("s", b, i))
                    release(dve.tensor_reduce(negm[:, t, h:h + 2], src[:, :].rearrange("p (h s) -> p h s", h=2), AX.X,
                                              ALU.max, negate=True), ("s", b, i))

            def split_maxima(b):
                read_out(dve, ("s", b, NSF - 1))
                read_out(dve, ("s", b, NSF - 2))
                if b >= 1:
                    full(dve, ("mT", b - 1))
                dve.tensor_copy(mparts[:, :, 0:NH], negm[:, :, :]).then_inc(mparts_done, 1)
                dve.wait_ge(mparts_done, 2 * b + 1)
                dve.tensor_tensor(mparts[:, :, NH:2 * NH], negm[:, :, :], mparts[:, :, 0:NH], ALU.subtract).then_inc(mparts_done, 1)

            def maxima_across(b):
                src = full(dve, ("mT", b))
                if b >= 2:
                    full(dve, ("st", b - 2, NH - 1))
                release(dve.tensor_copy(mT[:, b % 2, :], src[:, 0:S // 2].bitcast(BF16)), ("mT", b))

            def statistics(i, src, tiles=range(QT)):
                for t in tiles:
                    n = step(dve.bn_stats(stats[:, i, t, :], src[:, t, :]))
                for t in tiles:
                    after(n - tiles[-1] + t)
                    m = step(dve.bn_aggr(mv[:, i, t, :], stats[:, i, t, :]))
                after(m)
                dve.tensor_scalar(vare[:, i, tiles[0]:tiles[-1] + 1], mv[:, i, tiles[0]:tiles[-1] + 1, 1], LN_EPS, None,
                                  ALU.add).then_inc(ve_s[i], 1)

            def heads_out(b):
                for t in range(QT):
                    src = full(dve, ("avt", b, t))[:, :].rearrange("p (h s) -> p h s", h=NH)
                    n = step(dve.reciprocal(rsum[:, t, :], src[:, :, HD]))
                    after(n)
                    n = step(dve.tensor_scalar(rsum[:, t, :], rsum[:, t, :], scale3[:, 2:3], None, ALU.mult))
                    after(n)
                    if b >= 1 and t == 0:
                        full(dve, ("aT", b - 1))
                    release(dve.tensor_tensor(attn[:, t, :].rearrange("p (h d) -> p h d", h=NH), src[:, :, 0:HD],
                                              rsum[:, t, :].unsqueeze(2).broadcast_to((P, NH, HD)), ALU.mult), ("avt", b, t))

            def residual1(b):
                src = full(dve, ("op", b))
                dve.wait_ge(bias_added, NT)
                if b >= 1:
                    dve.wait_ge(yo_done, QT * (b - 1))
                release(dve.tensor_tensor(pre1[:, :, :], src[:, :].rearrange("p (t c) -> p t c", t=QT),
                                          x_sb[:, QT * b:QT * (b + 1), :], ALU.add), ("op", b))
                read_out(dve, ("op", b))
                statistics(0, pre1)

            def residual2(b):
                dve.wait_ge(rstd_s[0], b + 1)
                n = step(dve.tensor_scalar(rg[:, :], rstd[:, 0, :], gam[:, 4:5], None, ALU.mult))
                after(n)
                for t in range(QT):
                    n = step(dve.tensor_scalar(pre1[:, t, :], pre1[:, t, :], mv[:, 0, t, 0:1], rg[:, t:t + 1],
                                               ALU.subtract, ALU.mult))
                for t in range(QT):
                    after(n - QT + 1 + t)
                    m = step(dve.tensor_tensor(pre2[:, t, :], pre1[:, t, :], adjs[:, t, :], ALU.add))
                after(m)
                statistics(1, pre2)

            def norm2(b):
                dve.wait_ge(rstd_s[1], b + 1)
                for t in range(QT):
                    dve.tensor_scalar(x2[:, b % 2, t, :], pre2[:, t, :], mv[:, 1, t, 0:1], rstd[:, 1, t:t + 1],
                                      ALU.subtract, ALU.mult).then_inc(x2_done, 1)

            def x2_low(b):
                src = full(dve, ("x2t", b))
                dve.wait_ge(xhigh_done, b - SPLIT + 1)
                release(dve.tensor_tensor(x2low[:, :, :], src[:, :].rearrange("p (k s) -> p k s", k=KC),
                                          x2high[:, :, :].bitcast(F32), ALU.subtract), ("x2t", b))

            def hidden(b, f):
                n = b * NP2 + f
                dve.wait_ge(emptied["MG"], place[("g", b, f)][1] + 1)
                if n >= RING:
                    dve.wait_ge(hid_done, n - RING + 1)
                src = full(dve, ("u", b, f))
                release(dve.tensor_tensor(hid1[:, n % RING, :, :], src[:, :].rearrange("p (f s) -> p f s", f=2),
                                          silu[:, n % 2, :, :], ALU.mult), ("u", b, f))

            def experts_out(b, t):
                src = full(dve, ("y", b, t))
                release(dve.tensor_tensor(pre1[:, t, :], src[:, 0:C], x2[:, b % 2, t, :], ALU.add), ("y", b, t))
                read_out(dve, ("y", b, t))
                statistics(2, pre1, [t])
                dve.wait_ge(rstd_s[2], QT * b + t + 1)
                if b >= 2:
                    dve.wait_ge(out_done[b % 2], 16 * QT * (b // 2))
                dve.tensor_scalar(yo[:, b % 2, t, :], pre1[:, t, :], mv[:, 2, t, 0:1], rstd[:, 2, t:t + 1],
                                  ALU.subtract, ALU.mult).then_inc(yo_done, 1)

            def router_scores(b):
                src = full(dve, ("rt", b))[:, 0:QT * 16].rearrange("p (t n) -> p t n", t=QT)
                release(dve.tensor_copy(rsc[:, :, :], src[:, :, 0:NW]), ("rt", b))
                read_out(dve, ("rt", b))
                for t in range(QT):
                    n = step(dve.max(rtop[:, t, :], rsc[:, t, 0:NE]))
                dve.tensor_copy(rarg[:, :, 1], rsc[:, :, NE]).then_inc(rarg_done, 1)
                after(n)
                dve.tensor_tensor(rarg[:, :, 0], rtop[:, :, 0], rtop[:, :, 1], ALU.subtract).then_inc(rarg_done, 1)
                for t in range(QT):
                    n = step(dve.max_index(ridx[:, t, :], rtop[:, t, :], rsc[:, t, 0:NE]))
                after(n)
                return step(dve.tensor_copy(ridf[:, :, :], ridx[:, :, 0:2]))

            def router_weights(b, found):
                dve.wait_ge(rtanh_done, b + 1)
                dve.tensor_scalar(rw[:, :, :], rtanh[:, :, :], 0.5, 0.5, ALU.mult, ALU.add)
                n = step(dve.tensor_scalar(rw2[:, :, 0], rtanh[:, :, 0], -0.5, 0.5, ALU.mult, ALU.add))
                after(found)
                after(n)
                for t in range(QT):
                    for j in range(2):
                        w = rw[:, t, 0:1] if j == 0 else rw2[:, t, 0:1]
                        n = step(dve.tensor_scalar(hot[:, t, j, :], iota[:, :], ridf[:, t, j:j + 1], w, ALU.is_equal, ALU.mult))
                after(n)
                if b >= 1:
                    full(dve, ("cT", b - 1))
                dve.tensor_copy(comb[:, :, NE], rw[:, :, 1]).then_inc(comb_done, 1)
                dve.tensor_tensor(comb[:, :, 0:NE], hot[:, :, 0, :], hot[:, :, 1, :], ALU.add).then_inc(comb_done, 1)

            x_across(1)
            topk_rounds(0, 0, 3)
            x_across(3)
            for n in range(8):
                hf, kind, g = n // 4, (n // 2) % 2, n % 2
                m = abs_max(kind, 2 * hf + g, ("qk", n), qkraw[:, kind, g, hf * 512:(hf + 1) * 512])
                if n < 3:
                    topk_rounds(0, n + 3, n + 4)
                if n == 4:
                    gamma_step = gamma_factors()
            after(m)
            dve.tensor_reduce(amax3[:, 0:2], amax[:, 0:2, :], AX.X, ALU.max).then_inc(amax_done, 1)
            src = full(dve, ("mx", 0))
            release(dve.tensor_reduce(gmax[:, :], src[0:2, 0:P], AX.X, ALU.max), ("mx", 0))
            read_out(dve, ("mx", 0))
            dve.tensor_scalar(gdiag[:, :], ident[0:2, 0:2], gmax[:, 0:1], None, ALU.mult).then_inc(gmax_done, 1)
            m = abs_max(2, 0, ("v", 0), vraw[:, 0:2, :].rearrange("p t c -> p (t c)"))
            src = full(dve, ("mx", 1))
            release(dve.tensor_scalar(scale3[:, 0:2], src[:, 0:2], 1.0 / FP8_MAX, None, ALU.mult), ("mx", 1))
            read_out(dve, ("mx", 1))
            dve.reciprocal(inv3[:, 0:2], scale3[:, 0:2]).then_inc(scales_done, 1)
            n = step(dve.tensor_scalar(cexp[:, :], scale3[:, 0:1], HD ** -0.5, None, ALU.mult))
            after(n)
            dve.tensor_scalar(cexp[:, :], cexp[:, :], scale3[:, 1:2], None, ALU.mult).then_inc(scales_done, 1)
            quantize_first()
            spread_keys(0, 0, 0, 4)
            m = abs_max(2, 1, ("v", 1), vraw[:, 2:4, :].rearrange("p t c -> p (t c)"))
            m = abs_max(2, 2, ("v", 2), vraw[:, 4:6, :].rearrange("p t c -> p (t c)"))
            row_maxima(0, 0, 1)
            m = abs_max(2, 3, ("v", 3), vraw[:, 6:8, :].rearrange("p t c -> p (t c)"))
            after(m)
            dve.tensor_reduce(amax3[:, 2:3], amax[:, 2, :], AX.X, ALU.max).then_inc(amax_done, 1)
            src = full(dve, ("mx", 2))
            release(dve.tensor_reduce(gmaxv[:, :], src[0:1, 0:P], AX.X, ALU.max), ("mx", 2))
            row_maxima(0, 1, 2)
            src = full(dve, ("mx", 3))
            release(dve.tensor_scalar(scale3[:, 2:3], src[:, 0:1], 1.0 / FP8_MAX, None, ALU.mult), ("mx", 3))
            read_out(dve, ("mx", 3))
            dve.reciprocal(inv3[:, 2:3], scale3[:, 2:3]).then_inc(scales_done, 1)
            rounders(1, 1)
            row_maxima(0, 2, 3)
            row_maxima(0, 3, 10)
            rounders(1, 0)
            row_maxima(0, 10, NSF)
            split_maxima(0)
            maxima_across(0)
            rounders(0, 2)
            row_maxima(1, 0, 4)
            spread_keys(1, 1, 0, HG)
            row_maxima(1, 4, 8)
            topk_rounds(0, 6, 7)
            rounders(1, 2)
            row_maxima(1, 8, 12)
            topk_rounds(0, 7, 8)
            row_maxima(1, 12, NSF)
            split_maxima(1)
            maxima_across(1)

            for b in range(B):
                nxt, second, before = b + 1 < B, b + 2 < B, b > 0
                cuts = (0, 2, 4) if b == 0 else (0, 3, 5) if second else (0, 4, 6)
                if before and nxt:
                    maxima_across(b + 1)
                if nxt:
                    heads_out(b)
                    topk_rounds(b, last_round if before else 8, ROUNDS)
                    adjacency(b)
                last_round = cuts[2] + NP2 - 1
                if second:
                    rounders(b + 2, 1)
                if nxt:
                    topk_rounds(b + 1, cuts[0], cuts[1])
                    residual1(b)
                adjacency_sum(b)
                if second:
                    rounders(b + 2, 0)
                residual2(b)
                norm2(b)
                if second:
                    rounders(b + 2, 2)
                if b == 0:
                    spread_keys(b + 2, 0, 0, HG)
                if nxt:
                    topk_rounds(b + 1, cuts[1], cuts[1] + 1)
                if b >= SPLIT:
                    x2_low(b)
                if before:
                    experts_out(b - 1, 0)
                found = router_scores(b)
                router_weights(b, found)
                if before:
                    experts_out(b - 1, 1)
                if nxt:
                    topk_rounds(b + 1, cuts[1] + 1, cuts[2])
                for f in range(NP2):
                    if second:
                        row_maxima(b + 2, cuts_s[2 * f], cuts_s[2 * f + 1])
                    hidden(b, f)
                    if second:
                        row_maxima(b + 2, cuts_s[2 * f + 1], cuts_s[2 * f + 2])
                    elif nxt and f < 2:
                        topk_rounds(b + 1, cuts[2] + f, cuts[2] + f + 1)
                    elif nxt and f == 2:
                        heads_out(b + 1)
                    elif nxt and f == 3:
                        topk_rounds(b + 1, cuts[2] + 2, ROUNDS)
                        adjacency(b + 1)
                    elif nxt and f == NP2 - 1:
                        residual1(b + 1)
                    if second and f + 1 < NP2:
                        topk_rounds(b + 1, cuts[2] + f, cuts[2] + f + 1)
                if second:
                    split_maxima(b + 2)
            for t in range(QT):
                experts_out(B - 1, t)

        @block.tensor
        def _(pe):
            def transposes(key, pieces):
                dst = begin_fill(pe, key)
                for put, src in pieces:
                    ins = pe.transpose(put(dst), src, ident[0:src.shape[0], 0:src.shape[0]])
                end_fill(ins, key)

            def context_across(hf):
                pe.wait_ge(ld_ctx[hf], 16)
                transposes(("ct", hf), [(lambda d, j=j: d[0:D, j * P:(j + 1) * P], ctx_sb[:, 4 * hf + j, :]) for j in range(4)])

            def context_qk(hf):
                read_out(pe, ("ct", hf))
                for kind in range(2):
                    dst = begin_fill(pe, ("cq", kind, hf))
                    end_fill(pe.matmul(dst[:, :], wcT[:, kind, :], ctxT[:, hf * 512:(hf + 1) * 512], start=True, stop=True), ("cq", kind, hf))

            def similarities(b):
                read_out(pe, ("cq", 1, b // 2))
                read_out(pe, ("cq", 0, b // 2))
                dst = begin_fill(pe, ("sim", b))
                for t in range(QT):
                    tok = (QT * b + t) * P
                    ins = pe.matmul(dst[:, t * S:(t + 1) * S], qkcT[:, 0, tok:tok + P], qkcT[:, 1, b * S:(b + 1) * S], start=True, stop=True)
                end_fill(ins, ("sim", b))

            def x_across(n):
                pe.wait_ge(ld_x[n // 2], 16)
                transposes(("xt", n), [(lambda d, j=j: d[:, j * P:(j + 1) * P],
                                        x_sb[:, 4 * (n // 2) + j, (n % 2) * P:(n % 2 + 1) * P]) for j in range(4)])

            def queries_keys(n):
                hf, kind, g = n // 4, (n // 2) % 2, n % 2
                pe.wait_ge(ld_wqk, 16)
                for k in range(KC):
                    read_out(pe, ("xt", 2 * hf + k))
                dst = begin_fill(pe, ("qk", n))
                for k in range(KC):
                    ins = pe.matmul(dst[:, :], wqkv[:, k, kind * C + g * P:kind * C + (g + 1) * P],
                                    xT[:, k, hf * 512:(hf + 1) * 512], start=(k == 0), stop=(k == KC - 1))
                end_fill(ins, ("qk", n))

            def values(n):
                if n == 0:
                    pe.wait_ge(ld_wv, 16)
                dst = begin_fill(pe, ("v", n))
                for i in range(2):
                    tok = (2 * n + i) * P
                    for k in range(KC):
                        ins = pe.matmul(dst[:, i * C:(i + 1) * C], xT[:, k, tok:tok + P], wqkv[:, k, 2 * C:3 * C],
                                        start=(k == 0), stop=(k == KC - 1))
                end_fill(ins, ("v", n))

            def weights_across(n):
                which, pieces = n // (NWT // 3), []
                if n % (NWT // 3) == 0:
                    pe.wait_ge((ld_wg, ld_wu, ld_wd)[which], 64 if which == 2 else 32)
                for j in range(4):
                    s = 4 * (n % (NWT // 3)) + j
                    if which < 2:
                        src = (wg_nat, wu_nat)[which][:, s % NF, (s // NF) * P:(s // NF + 1) * P]
                    else:
                        src = wd_nat[:, s % KC, s // KC, :]
                    pieces.append((lambda d, j=j: d[:, j * P:(j + 1) * P], src))
                transposes(("wt", n), pieces)

            def adjacency_transposes(b):
                pe.wait_ge(adj_done, QT * (b + 1))
                transposes(("at", b), [(lambda d, i=i, j=j: d[:, i * S + j * P:i * S + (j + 1) * P], adj[:, j, i * P:(i + 1) * P])
                                       for i in range(QT) for j in range(QT)])

            def query_scores(b, first, last):
                if first == 0:
                    pe.wait_ge(quantized[0], b + 1)
                for i in range(first, last):
                    g, t, hp = i // (2 * HG // 2), (i // (HG // 2)) % 2, i % (HG // 2)
                    if t == 0:
                        pe.wait_ge(km_done[g], HG * b + 2 * hp + 2)
                    h = g * HG + 2 * hp
                    dst = begin_fill(pe, ("s", b, i))
                    end_fill(pe.matmul(dst[:, :], q8[:, b % 2, g, t * P:(t + 1) * P], kmask[:, b % 2, h:h + 2, :],
                                       start=True, stop=True), ("s", b, i))

            def maxima_across(b):
                pe.wait_ge(mparts_done, 2 * (b + 1))
                pe.wait_ge(consts, 9)
                dst = begin_fill(pe, ("mT", b))
                for t in range(QT):
                    ins = pe.transpose(dst[:, t * P // 2:(t + 1) * P // 2].bitcast(BF16), mparts[:, t, :], identb[:, :])
                end_fill(ins, ("mT", b))

            def key_scores(b, h):
                dst = begin_fill(pe, ("st", b, h))
                for t in range(QT):
                    pe.matmul(dst[:, t * S:(t + 1) * S], kmask[:, b % 2, h, t * P:(t + 1) * P], q8[:, b % 2, h // HG, :],
                              start=True, stop=False)
                    ins = pe.matmul(dst[:, t * S:(t + 1) * S], sel[:, h, :], mT[:, b % 2, :], start=False, stop=True)
                end_fill(ins, ("st", b, h))

            def attend(b, grp):
                key = ("av", b, grp // 2)
                dst = begin_fill(pe, key) if grp % 2 == 0 else bank[place[key][0]]
                if grp == 0:
                    pe.wait_ge(quantized[2], b + 1)
                for h in range(4 * grp + 2, 4 * grp + 4):
                    read_out(pe, ("st", b, h))
                for t in range(QT):
                    for j in range(4):
                        h = 4 * grp + j
                        ins = pe.matmul(dst[SLOT * j:SLOT * (j + 1), (grp % 2) * S:(grp % 2 + 1) * S], v8[:, b % 2, t, h, :],
                                        expo[:, h % ER, t, :], start=(t == 0), stop=(t == QT - 1))
                if grp % 2:
                    end_fill(ins, key)
                else:
                    ins.then_inc(av_half, 1)

            def heads_across(b):
                read_out(pe, ("av", b, 1))
                for t in range(QT):
                    transposes(("avt", b, t), [(lambda d, g=g: d[:, g * P:(g + 1) * P], avT[:, g, t * P:(t + 1) * P])
                                               for g in range(NG)])

            def attention_across(b):
                for t in range(QT):
                    read_out(pe, ("avt", b, t))
                transposes(("aT", b), [(lambda d, k=k, t=t: d[:, k * S + t * P:k * S + (t + 1) * P], attn[:, t, k * P:(k + 1) * P])
                                       for k in range(KC) for t in range(QT)])

            def project(b):
                read_out(pe, ("aT", b))
                pe.wait_ge(ld_wout, 16)
                dst = begin_fill(pe, ("op", b))
                for t in range(QT):
                    for k in range(KC):
                        ins = pe.matmul(dst[:, t * C:(t + 1) * C], aT[:, k, t * P:(t + 1) * P], wout[:, k, :],
                                        start=(k == 0), stop=(k == KC - 1))
                end_fill(ins, ("op", b))

            def experts_in(b, f, name, w, high, low):
                dst = begin_fill(pe, (name, b, f))
                if b == SPLIT and f == 0:
                    pe.wait_ge(wlow_done, NWG)
                for i in range(2):
                    if b < SPLIT:
                        terms = [(w[:, k, 2 * f + i, :], x2T[:, b % 2, k, :]) for k in range(KC)]
                    else:
                        terms = [(a[:, k, 2 * f + i, :], part[:, k, :])
                                 for k in range(KC) for a, part in ((high, x2high), (high, x2low), (low, x2high))]
                    for n, (a, c) in enumerate(terms):
                        ins = pe.matmul(dst[:, i * S:(i + 1) * S], a, c, start=(n == 0), stop=(n == len(terms) - 1))
                end_fill(ins, (name, b, f))

            def experts_out(b, t, first, last):
                key = ("y", b, t)
                dst = begin_fill(pe, key) if first == 0 else bank[place[key][0]]
                if b == 0 and t == 0 and first == 0:
                    read_out(pe, ("wt", NWT - 1))
                    read_out(pe, ("wt", NWT - 2))
                for f in range(first, last):
                    if t == 0 and f % 2 == 0:
                        pe.wait_ge(hid_done, NP2 * b + f // 2 + 1)
                    ins = pe.matmul(dst[:, 0:C], hid[:, f, t * P:(t + 1) * P], wdT[:, f, :],
                                    start=(f == 0), stop=(f == NF - 1))
                if last == NF:
                    end_fill(ins, key)

            def tokens_across(b):
                pe.wait_ge(x2_done, QT * (b + 1))
                transposes(("x2t", b), [(lambda d, k=k, t=t: d[:, k * S + t * P:k * S + (t + 1) * P], x2[:, b % 2, t, k * P:(k + 1) * P])
                                        for k in range(KC) for t in range(QT)])

            def route(b):
                read_out(pe, ("x2t", b))
                dst = begin_fill(pe, ("rt", b))
                parts = [x2T[:, b % 2]] if b < SPLIT else [x2high[:].bitcast(F32), x2low[:].bitcast(F32)]
                for t in range(QT):
                    for k in range(KC):
                        for n, part in enumerate(parts):
                            ins = pe.matmul(dst[:, t * 16:t * 16 + NW], part[:, k, t * P:(t + 1) * P], gwT[:, k, :],
                                            start=(k == 0 and n == 0), stop=(k == KC - 1 and n == len(parts) - 1))
                end_fill(ins, ("rt", b))

            def route_across(b):
                pe.wait_ge(comb_done, 2 * (b + 1))
                transposes(("cT", b), [(lambda d, t=t: d[0:NW, t * P:(t + 1) * P], comb[:, t, :]) for t in range(QT)])

            def great_transpose(n, src):
                pe.wait_ge(amax_done, n // 2 + 1)
                dst = begin_fill(pe, ("mx", n))
                end_fill(pe.transpose(dst[0:src.shape[1], 0:P], src, ident[:, :]), ("mx", n))

            pe.wait_ge(warm_set, 1)
            for n in range(WARM):
                pe.matmul(bank["SA0"][:, :], warm[:, 0:P], warm, start=True, stop=True)
            pe.wait_ge(consts, 3)
            pe.wait_ge(ld_wc, 32)
            transposes(("cw",), [(lambda d, k=k: d[0:D, k * D:(k + 1) * D], wc_sb[:, k, :]) for k in range(2)])
            context_across(0)
            read_out(pe, ("cw",))
            context_qk(0)
            x_across(0)
            x_across(1)
            similarities(0)
            queries_keys(0)
            similarities(1)
            queries_keys(1)
            x_across(2)
            x_across(3)
            for n in range(2, 8):
                queries_keys(n)
            values(0)
            great_transpose(0, amax3[:, 0:2])
            context_across(1)
            pe.wait_ge(gmax_done, 1)
            pe.wait_ge(consts, 7)
            dst = begin_fill(pe, ("mx", 1))
            end_fill(pe.matmul(dst[:, 0:2], ones[0:2, :], gdiag[:, :], start=True, stop=True), ("mx", 1))
            for n in range(1, 4):
                values(n)
            context_qk(1)
            query_scores(0, 0, 2)
            similarities(2)
            great_transpose(2, amax3[:, 2:3])
            read_out(pe, ("mx", 2))
            dst = begin_fill(pe, ("mx", 3))
            end_fill(pe.matmul(dst[:, 0:1], ones[0:1, :], gmaxv[:, :], start=True, stop=True), ("mx", 3))
            query_scores(0, 2, 4)
            similarities(3)
            for n in range(NWG):
                weights_across(n)
                query_scores(0, 4 + n, 5 + n)
            query_scores(0, 4 + NWG, NSF)
            maxima_across(0)
            for n in range(NWG):
                read_out(pe, ("wt", n))
            read_out(pe, ("mT", 0))
            for grp in range(NG):
                for j in range(4):
                    key_scores(0, 4 * grp + j)
                    query_scores(1, 4 * grp + j, 4 * grp + j + 1)
                if grp > 0:
                    attend(0, grp - 1)
            attend(0, NG - 1)
            maxima_across(1)

            ACROSS, PROJECT = 3, 7
            COVER = 3
            HELD = (3, 2)
            LAG = 3
            for b in range(B):
                nxt, second, before = b + 1 < B, b + 2 < B, b > 0

                def scores_and_filling(h):
                    if nxt:
                        key_scores(b + 1, h)
                    if before:
                        done = COVER if nxt else 0
                        todo = QT * NF - done - sum(HELD)
                        for m in range(done + todo * h // NH, done + todo * (h + 1) // NH):
                            experts_out(b - 1, m // NF, m % NF, m % NF + 1)
                    elif h == 3:
                        pe.wait_ge(ld_gw, 32)
                        transposes(("gw",), [(lambda d, k=k: d[:, k * 16:k * 16 + NW], gw_nat[:, k * P:(k + 1) * P]) for k in range(KC)])
                        weights_across(NWG)
                    elif h == 7 or h == 11:
                        weights_across(NWG + h // 4)
                    elif h == 15:
                        weights_across(NWG + 3)
                        weights_across(NWG + 4)

                if nxt:
                    heads_across(b)
                if before and nxt:
                    experts_out(b - 1, 0, 0, 1)
                    maxima_across(b + 1)
                    experts_out(b - 1, 0, 1, COVER)
                if nxt:
                    read_out(pe, ("mT", b + 1))
                for h in range(NH):
                    scores_and_filling(h)
                    if nxt and h == ACROSS:
                        attention_across(b)
                    if nxt and h == PROJECT:
                        project(b)
                        adjacency_transposes(b)
                    if nxt and h in (7, 11):
                        attend(b + 1, h // 4 - 1)
                tokens_across(b)
                if nxt:
                    attend(b + 1, 2)
                if before:
                    experts_out(b - 1, 1, NF - sum(HELD), NF - HELD[1])
                if b == 0:
                    read_out(pe, ("gw",))
                route(b)
                if before:
                    experts_out(b - 1, 1, NF - HELD[1], NF)
                if nxt:
                    attend(b + 1, 3)
                for f in range(NP2):
                    experts_in(b, f, "g", wgT, wghigh, wglow)
                    if f == 0:
                        route_across(b)
                    if second:
                        query_scores(b + 2, cuts_s[2 * f], cuts_s[2 * f + 1])
                    elif nxt and f == 3:
                        heads_across(b + 1)
                    elif nxt and f == 4:
                        project(b + 1)
                        adjacency_transposes(b + 1)
                    experts_in(b, f, "u", wuT, wuhigh, wulow)
                    if second:
                        query_scores(b + 2, cuts_s[2 * f + 1], cuts_s[2 * f + 2])
                    elif nxt and f == 3:
                        attention_across(b + 1)
                    if not nxt and f >= LAG:
                        for t in range(QT):
                            experts_out(b, t, 2 * (f - LAG), 2 * (f - LAG) + 2)
            for f in range(NP2 - LAG, NP2):
                for t in range(QT):
                    experts_out(B - 1, t, 2 * f, 2 * f + 2)


_INS = ['x', 'ctx_512', 'L0_attn_W_qkv', 'L0_attn_W_out', 'L0_attn_b_out', 'L0_xattn_Wq', 'L0_xattn_Wk',
        'L0_xattn_gamma_raw', 'L0_ffn_gate_w', 'L0_ffn_w_gate', 'L0_ffn_w_up', 'L0_ffn_w_down',
        'L0_ffn_sh_gate', 'L0_ffn_sh_up', 'L0_ffn_sh_down', 'L0_ffn_se_gate_w']
_OUTS = [((4, 256, 256), 'float32')]


def kernel(**inputs):
    import numpy as _np
    import concourse.bacc as _bacc
    from concourse import mybir as _mybir
    from concourse.bass_utils import run_bass_kernel_spmd as _run

    nc = _bacc.Bacc("TRN2", target_bir_lowering=False, num_devices=1)
    arrays, args = {}, []
    for name in _INS:
        a = _np.ascontiguousarray(inputs[name])
        arrays[f"in_{name}_dram"] = a
        args.append(nc.dram_tensor(f"in_{name}_dram", a.shape, _mybir.dt.from_np(a.dtype), kind="ExternalInput").ap())
    for i, (shape, dtype) in enumerate(_OUTS):
        dt = _mybir.dt.from_np(_np.dtype(dtype))
        args.append(nc.dram_tensor(f"out_{i}_dram", shape, dt, kind="ExternalOutput").ap())
    decoder_layer(nc, *args)
    r = _run(nc, [arrays], core_ids=[0])
    return r.results[0]["out_0_dram"]
```
